# Optimizing a Trainium2 kernel written in Bass

```python
import numpy as np
import jax
import jax.numpy as jnp

def _softmax(x, axis=-1):
    return jax.nn.softmax(x, axis=axis)

def _gelu(x):
    return jax.nn.gelu(x, approximate=True)

def _silu(x):
    return jax.nn.silu(x)

def _sigmoid(x):
    return jax.nn.sigmoid(x)

def _layernorm(x, axis=-1, eps=1e-05):
    m = jnp.mean(x, axis=axis, keepdims=True)
    v = jnp.var(x, axis=axis, keepdims=True)
    return (x - m) / jnp.sqrt(v + eps)

def _scatter_add(tgt, idx, src, axis=0):
    return tgt.at[idx].add(src)

def _segment_sum(src, seg, n):
    return jax.ops.segment_sum(src, seg, n)
kernel_name = 'mk_adaln_d1_jaxref_r8_e2c904'

def setup_inputs(seed: int=0):
    np.random.seed(seed)
    _w = jnp.asarray

    def _L0_attn_setup():
        import jax, jax.numpy as jnp
        import numpy as np
        B, N, D_MODEL = (2, 512, 256)
        H = 4
        KEY_DIM = 128
        DK = KEY_DIM // H
        DV = D_MODEL // H
        CHUNK = 64
        EPS = 1e-05

        def _rope(qk):
            n, d = (qk.shape[1], qk.shape[3])
            inv_freq = 1.0 / 10000.0 ** (jnp.arange(0, d, 2, dtype=jnp.float32) / d)
            freqs = jnp.arange(n, dtype=jnp.float32)[:, None] * inv_freq[None, :]
            cos = jnp.cos(freqs)[None, :, None, :]
            sin = jnp.sin(freqs)[None, :, None, :]
            x1, x2 = (qk[..., :d // 2], qk[..., d // 2:])
            return jnp.concatenate([x1 * cos - x2 * sin, x2 * cos + x1 * sin], axis=-1)

        def _retention_forward(x, Wq, Wk, Wv, Wg, Wo, gnorm_w):
            b, n, dm = x.shape
            dk, dv = (Wq.shape[0] // H, Wv.shape[0] // H)
            q = (x @ Wq.T).reshape(b, n, H, dk)
            k = (x @ Wk.T).reshape(b, n, H, dk)
            q, k = (_rope(q), _rope(k))
            v = (x @ Wv.T).reshape(b, n, H, dv)
            q = q.transpose(0, 2, 1, 3) * dk ** (-0.5)
            k = k.transpose(0, 2, 1, 3)
            v = v.transpose(0, 2, 1, 3)
            gamma = 1.0 - jnp.exp2(-5.0 - jnp.arange(H, dtype=jnp.float32))
            C = CHUNK
            nc = n // C
            qc = q.reshape(b, H, nc, C, dk).transpose(2, 0, 1, 3, 4)
            kc = k.reshape(b, H, nc, C, dk).transpose(2, 0, 1, 3, 4)
            vc = v.reshape(b, H, nc, C, dv).transpose(2, 0, 1, 3, 4)
            i = jnp.arange(C)
            expo = (i[:, None] - i[None, :]).astype(jnp.float32)
            dmask = jnp.where(expo >= 0, gamma[:, None, None] ** expo, 0.0)
            g_in = gamma[:, None] ** (i + 1).astype(jnp.float32)
            g_k = gamma[:, None] ** (C - 1 - i).astype(jnp.float32)
            g_C = gamma ** C

            def step(S, inp):
                qi, ki, vi = inp
                attn = jnp.einsum('bhid,bhjd->bhij', qi, ki) * dmask[None]
                o_intra = jnp.einsum('bhij,bhjv->bhiv', attn, vi)
                o_inter = jnp.einsum('bhid,bhdv->bhiv', qi, S) * g_in[None, :, :, None]
                S_new = S * g_C[None, :, None, None] + jnp.einsum('bhjd,bhjv->bhdv', ki * g_k[None, :, :, None], vi)
                return (S_new, o_intra + o_inter)
            S0 = jnp.zeros((b, H, dk, dv), x.dtype)
            _, oc = jax.lax.scan(step, S0, (qc, kc, vc))
            o = oc.transpose(1, 0, 3, 2, 4).reshape(b, n, H, dv)
            o = o * jax.lax.rsqrt(jnp.mean(o * o, axis=-1, keepdims=True) + EPS) * gnorm_w
            g = jax.nn.silu(x @ Wg.T)
            return o.reshape(b, n, H * dv) * g @ Wo.T
        key = jax.random.key(seed)
        ks = jax.random.split(key, 6)
        s = 0.02
        return {'x': jax.random.normal(ks[0], (B, N, D_MODEL), jnp.float32), 'Wq': jax.random.normal(ks[1], (KEY_DIM, D_MODEL), jnp.float32) * s, 'Wk': jax.random.normal(ks[2], (KEY_DIM, D_MODEL), jnp.float32) * s, 'Wv': jax.random.normal(ks[3], (D_MODEL, D_MODEL), jnp.float32) * s, 'Wg': jax.random.normal(ks[4], (D_MODEL, D_MODEL), jnp.float32) * s, 'Wo': jax.random.normal(ks[5], (D_MODEL, D_MODEL), jnp.float32) * s, 'gnorm_w': jnp.ones((DV,), jnp.float32)}
    _L0_attn_in = _L0_attn_setup()

    def _L0_ffn_setup():
        import jax, jax.numpy as jnp
        import numpy as np
        B, S, D, H = (4, 256, 256, 1024)

        def fwht(x):
            orig_shape = x.shape
            n = orig_shape[-1]
            x = x.reshape(-1, n)
            h = 1
            while h < n:
                xb = x.reshape(-1, n // (2 * h), 2, h)
                a = xb[:, :, 0, :]
                b = xb[:, :, 1, :]
                x = jnp.stack([a + b, a - b], axis=2).reshape(-1, n)
                h *= 2
            scale = jnp.asarray(1.0 / np.sqrt(n), dtype=x.dtype)
            return (x * scale).reshape(orig_shape)
        key = jax.random.key(seed)
        kx, k1, k2, k3 = jax.random.split(key, 4)
        x = jax.random.normal(kx, (B, S, D), dtype=jnp.float32)
        W1 = jax.random.normal(k1, (H, D), dtype=jnp.float32) * (1.0 / np.sqrt(D))
        W2 = jax.random.normal(k2, (D, H), dtype=jnp.float32) * (1.0 / np.sqrt(H))
        W3 = jax.random.normal(k3, (H, D), dtype=jnp.float32) * (1.0 / np.sqrt(D))
        return {'x': x, 'W1': W1, 'W2': W2, 'W3': W3}
    _L0_ffn_in = _L0_ffn_setup()
    _L0_c = _w((lambda *s: np.random.randn(*s).astype(np.float32) * 0.05)(4, 256))
    _L0_wmod = _w((lambda *s: np.random.randn(*s).astype(np.float32) * 0.05)(256, 6 * 256) * 256 ** (-0.5))
    _d = {'L0_attn_x': _L0_attn_in['x'], 'L0_attn_Wq': _L0_attn_in['Wq'], 'L0_attn_Wk': _L0_attn_in['Wk'], 'L0_attn_Wv': _L0_attn_in['Wv'], 'L0_attn_Wg': _L0_attn_in['Wg'], 'L0_attn_Wo': _L0_attn_in['Wo'], 'L0_attn_gnorm_w': _L0_attn_in['gnorm_w'], 'L0_ffn_W1': _L0_ffn_in['W1'], 'L0_ffn_W2': _L0_ffn_in['W2'], 'L0_ffn_W3': _L0_ffn_in['W3'], 'L0_c': _L0_c, 'L0_wmod': _L0_wmod}
    _x0 = _d['L0_attn_x']
    _d['L0_attn_x'] = jax.random.normal(jax.random.fold_in(jax.random.key(seed), 1), (4, 512, 256), dtype=_x0.dtype)
    del _x0
    return _d

def reference(L0_attn_x, L0_attn_Wq, L0_attn_Wk, L0_attn_Wv, L0_attn_Wg, L0_attn_Wo, L0_attn_gnorm_w, L0_ffn_W1, L0_ffn_W2, L0_ffn_W3, L0_c, L0_wmod):

    def _L0_attn_ref(x, Wq, Wk, Wv, Wg, Wo, gnorm_w):
        import jax, jax.numpy as jnp
        import numpy as np
        B, N, D_MODEL = (2, 512, 256)
        H = 4
        KEY_DIM = 128
        DK = KEY_DIM // H
        DV = D_MODEL // H
        CHUNK = 64
        EPS = 1e-05

        def _rope(qk):
            n, d = (qk.shape[1], qk.shape[3])
            inv_freq = 1.0 / 10000.0 ** (jnp.arange(0, d, 2, dtype=jnp.float32) / d)
            freqs = jnp.arange(n, dtype=jnp.float32)[:, None] * inv_freq[None, :]
            cos = jnp.cos(freqs)[None, :, None, :]
            sin = jnp.sin(freqs)[None, :, None, :]
            x1, x2 = (qk[..., :d // 2], qk[..., d // 2:])
            return jnp.concatenate([x1 * cos - x2 * sin, x2 * cos + x1 * sin], axis=-1)

        def _retention_forward(x, Wq, Wk, Wv, Wg, Wo, gnorm_w):
            b, n, dm = x.shape
            dk, dv = (Wq.shape[0] // H, Wv.shape[0] // H)
            q = (x @ Wq.T).reshape(b, n, H, dk)
            k = (x @ Wk.T).reshape(b, n, H, dk)
            q, k = (_rope(q), _rope(k))
            v = (x @ Wv.T).reshape(b, n, H, dv)
            q = q.transpose(0, 2, 1, 3) * dk ** (-0.5)
            k = k.transpose(0, 2, 1, 3)
            v = v.transpose(0, 2, 1, 3)
            gamma = 1.0 - jnp.exp2(-5.0 - jnp.arange(H, dtype=jnp.float32))
            C = CHUNK
            nc = n // C
            qc = q.reshape(b, H, nc, C, dk).transpose(2, 0, 1, 3, 4)
            kc = k.reshape(b, H, nc, C, dk).transpose(2, 0, 1, 3, 4)
            vc = v.reshape(b, H, nc, C, dv).transpose(2, 0, 1, 3, 4)
            i = jnp.arange(C)
            expo = (i[:, None] - i[None, :]).astype(jnp.float32)
            dmask = jnp.where(expo >= 0, gamma[:, None, None] ** expo, 0.0)
            g_in = gamma[:, None] ** (i + 1).astype(jnp.float32)
            g_k = gamma[:, None] ** (C - 1 - i).astype(jnp.float32)
            g_C = gamma ** C

            def step(S, inp):
                qi, ki, vi = inp
                attn = jnp.einsum('bhid,bhjd->bhij', qi, ki) * dmask[None]
                o_intra = jnp.einsum('bhij,bhjv->bhiv', attn, vi)
                o_inter = jnp.einsum('bhid,bhdv->bhiv', qi, S) * g_in[None, :, :, None]
                S_new = S * g_C[None, :, None, None] + jnp.einsum('bhjd,bhjv->bhdv', ki * g_k[None, :, :, None], vi)
                return (S_new, o_intra + o_inter)
            S0 = jnp.zeros((b, H, dk, dv), x.dtype)
            _, oc = jax.lax.scan(step, S0, (qc, kc, vc))
            o = oc.transpose(1, 0, 3, 2, 4).reshape(b, n, H, dv)
            o = o * jax.lax.rsqrt(jnp.mean(o * o, axis=-1, keepdims=True) + EPS) * gnorm_w
            g = jax.nn.silu(x @ Wg.T)
            return o.reshape(b, n, H * dv) * g @ Wo.T
        return _retention_forward(x, Wq, Wk, Wv, Wg, Wo, gnorm_w)

    def _L0_ffn_ref(x, W1, W2, W3):
        import jax, jax.numpy as jnp
        import numpy as np
        B, S, D, H = (4, 256, 256, 1024)

        def fwht(x):
            orig_shape = x.shape
            n = orig_shape[-1]
            x = x.reshape(-1, n)
            h = 1
            while h < n:
                xb = x.reshape(-1, n // (2 * h), 2, h)
                a = xb[:, :, 0, :]
                b = xb[:, :, 1, :]
                x = jnp.stack([a + b, a - b], axis=2).reshape(-1, n)
                h *= 2
            scale = jnp.asarray(1.0 / np.sqrt(n), dtype=x.dtype)
            return (x * scale).reshape(orig_shape)
        up_gate = jnp.einsum('bsd,hd->bsh', x, W1)
        up_lin = jnp.einsum('bsd,hd->bsh', x, W3)
        hidden = jax.nn.silu(up_gate) * up_lin
        hidden = fwht(hidden)
        out = jnp.einsum('bsh,dh->bsd', hidden, W2)
        return out
    x = L0_attn_x
    mod = (_silu(L0_c) @ L0_wmod).reshape(L0_c.shape[0], 6, 1, -1)
    sa, ca, ga, sb, cb, gb = (mod[:, 0], mod[:, 1], mod[:, 2], mod[:, 3], mod[:, 4], mod[:, 5])
    ga = (2 * (ga >= 0) - 1) * jnp.maximum(jnp.abs(ga), 0.25)
    gb = (2 * (gb >= 0) - 1) * jnp.maximum(jnp.abs(gb), 0.25)
    h = _layernorm(x, axis=-1) * (1 + ca) + sa
    x = x + ga * _L0_attn_ref(h, L0_attn_Wq, L0_attn_Wk, L0_attn_Wv, L0_attn_Wg, L0_attn_Wo, L0_attn_gnorm_w)
    h = _layernorm(x, axis=-1) * (1 + cb) + sb
    x = x + gb * _L0_ffn_ref(h, L0_ffn_W1, L0_ffn_W2, L0_ffn_W3)
    return x

_drawn_inputs = setup_inputs


def setup_inputs(seed=0):
    import zlib

    import numpy as np

    out = dict(_drawn_inputs(seed))
    spreads = {'L0_attn_gnorm_w': (1.0, 0.6)}
    factors = {'L0_attn_Wq': 4.004,
     'L0_attn_Wk': 3.987,
     'L0_attn_Wv': 3.97,
     'L0_attn_Wg': 4.022,
     'L0_attn_Wo': 4.001}
    for name, (base, spread) in spreads.items():
        noise = np.random.default_rng([zlib.crc32(name.encode()), seed]).standard_normal(out[name].shape)
        drawn = base * np.exp(spread * noise) if base else spread * noise
        out[name] = jnp.asarray(drawn.astype(out[name].dtype))
    for name, factor in factors.items():
        out[name] = (out[name] * factor).astype(out[name].dtype)
    return out
```

```python
from contextlib import ExitStack

import numpy as np

import concourse.bass as bass
from concourse import mybir

P = 128
B, N, D = 4, 512, 256
HEADS, DK, DV = 4, 32, 64
HID = 1024
TILES = N // P
KC = D // P
QK = 2 * HEADS * DK
VG = 2 * HEADS * DV
HB = HID // P
PIECES = 4
PW = HID // PIECES
EPS = 1e-5
MIN_GATE = 0.25
SA, CA, GA, SB, CB, GB = range(6)

F32 = mybir.dt.float32
F32R = mybir.dt.float32r
ALU = mybir.AluOpType
ACT = mybir.ActivationFunctionType
AX = mybir.AxisListType

C_IDENT, C_CAUSAL, C_HADAMARD, C_BLOCKS, C_END = 0, P, 2 * P, 3 * P, 3 * P + HEADS * DV


def steps(text):
    return [(w[0], int(w[1])) for w in text.split()]


FIRST = steps("R0 T0 M0 J0 X0 G0 P0 P1 P2 P3 J1 X1 Q0 X2 J2 G1 S0 K0 S1 R1 K1 S2 O0 S3 K2 X3 O1 V0 N0 O2 O3 X4 Y0 "
              "N1 H0 Y1 W0 W1 L0 R2 R3")
STEADY = steps("U0 T0 U1 P0 P1 D0 P2 P3 U2 Q0 U3 D1 S0 K0 D2 S1 D3 K1 S2 O0 K2 S3 O1 O2 N0 U4 O3 N1 Y0 U5 Y1 W0 U6 "
               "W1 D4 U7 D5 L0 D6 D7 F0")
LAST = steps("U0 U1 U2 D0 U3 D1 U4 D2 U5 D3 U6 D4 U7 D5 D6 D7 F0")


class Signal:

    def __init__(self, sem, per):
        self.sem, self.per = sem, per

    def after(self, batch, k):
        return batch * self.per + k


def adaln_block_kernel(nc, x, c_t, w_qkvg, w_o, gnorm, w13, w2, wmod, consts, select, cos, sin, out):
    with ExitStack() as ctx:
        def sb(name, shape, dt=F32, scope=ctx):
            return scope.enter_context(nc.sbuf_tensor(name, shape, dt))

        def bank(name):
            return ctx.enter_context(nc.psum_tensor(name, [P, 512], F32))

        def sem(name, per=0):
            return Signal(ctx.enter_context(nc.semaphore(name)), per)

        xres = sb("xres", [P, B, TILES, D])
        mod_cols = sb("mod_cols", [P, B, 4, KC])
        gates = sb("gates", [P, B, 2, D])
        cst = sb("cst", [P, C_END])
        ident, causal = cst[:, C_IDENT:C_IDENT + P], cst[:, C_CAUSAL:C_CAUSAL + P]
        hadamard, blocks = cst[:, C_HADAMARD:C_HADAMARD + P], cst[:, C_BLOCKS:C_END]
        had_r = sb("had_r", [P, P], F32R)
        cos_sb, sin_sb = sb("cos_sb", [P, TILES, QK]), sb("sin_sb", [P, TILES, QK])
        gnorm_in, gnorm_sb = sb("gnorm_in", [P, DV]), sb("gnorm_sb", [P, DV])
        mhalf = sb("mhalf", [P, 2 * HEADS])
        eps_ln, eps_rms = sb("eps_ln", [P, TILES]), sb("eps_rms", [P, 2 * HEADS])
        c_sb, sc_sb = sb("c_sb", [P, KC, B]), sb("sc_sb", [P, KC, B])
        mv1 = sb("mv1", [P, B, TILES, 2])
        ve1, rs1 = sb("ve1", [P, B, TILES]), sb("rs1", [P, B, TILES])
        wqkvg_hi, wqkvg_lo = (sb("wqkvg_" + e, [P, KC, QK + VG], F32R) for e in ("hi", "lo"))
        wo_hi, wo_lo = (sb("wo_" + e, [P, KC, D], F32R) for e in ("hi", "lo"))
        w13_hi, w13_lo = (sb("w13_" + e, [P, PIECES, 2, KC, PW], F32R) for e in ("hi", "lo"))

        stats1, stats = sb("stats1", [P, TILES, 6]), sb("stats", [P, TILES, 6])
        mv_cur, rs_cur = sb("mv_cur", [P, TILES, 2]), sb("rs_cur", [P, TILES])
        mod_cur = sb("mod_cur", [P, 4, KC])
        mv2, ve2, rs2 = sb("mv2", [P, TILES, 2]), sb("ve2", [P, TILES]), sb("rs2", [P, TILES])
        xn = sb("xn", [P, TILES, D])
        h32 = sb("h32", [P, KC, N])
        p32 = h32[:, :, :].rearrange("p k (h i) -> p k h i", h=HEADS)
        h1_hi, h1_lo = sb("h1_hi", [P, KC, N], F32R), sb("h1_lo", [P, KC, N], F32R)
        rope_a, rope_b = sb("rope_a", [P, 2, QK]), sb("rope_b", [P, 2, QK])
        qk = sb("qk", [P, TILES, QK])
        x1 = qk
        k_hi, k_lo = sb("k_hi", [P, TILES, P], F32R), sb("k_lo", [P, TILES, P], F32R)
        v_hi, v_lo = sb("v_hi", [P, TILES, D], F32R), sb("v_lo", [P, TILES, D], F32R)
        gg = sb("gg", [P, TILES, D])
        qt_hi, qt_lo = sb("qt_hi", [P, TILES, P], F32R), sb("qt_lo", [P, TILES, P], F32R)
        kt_hi, kt_lo = sb("kt_hi", [P, TILES, P], F32R), sb("kt_lo", [P, TILES, P], F32R)
        p_hi, p_lo = sb("p_hi", [P, 2, HEADS, P], F32R), sb("p_lo", [P, 2, HEADS, P], F32R)
        s32 = sb("s32", [P, HEADS * DV])
        s_hi, s_lo = sb("s_hi", [P, 2, HEADS * DV], F32R), sb("s_lo", [P, 2, HEADS * DV], F32R)
        sq = sb("sq", [P, 2, D])
        ss, vo, rso = (sb(n, [P, TILES, HEADS]) for n in ("ss", "vo", "rso"))
        tmp = sb("tmp", [P, 2, D])

        gate_row = tmp[0:B].rearrange("b g d -> b (g d)")
        gate_size = sq[0:B].rearrange("b g d -> b (g d)")

        with ExitStack() as scope:
            fly0 = sb("fly0", [P, HB, D], scope=scope)
        w2_hi = sb("w2_hi", [P, HB, D], F32R)
        w2_lo = sb("w2_lo", [P, HB, D], F32R)
        with ExitStack() as scope:
            wmod_sb = sb("wmod_sb", [P, KC, 6 * D], scope=scope)
            stage_qkvg = sb("stage_qkvg", [P, KC, QK + VG], scope=scope)
        qb_hi = sb("qb_hi", [P, TILES, HEADS, P], F32R)
        qb_lo = sb("qb_lo", [P, TILES, HEADS, P], F32R)
        g32 = sb("g32", [P, 2, D])
        with ExitStack() as scope:
            fly1 = sb("fly1", [P, HB, D], scope=scope)
            stage_13 = sb("stage_13", [P, 2, 2, KC, PW], scope=scope)
            stage_wo = sb("stage_wo", [P, KC, D], scope=scope)
            sel_sb = sb("sel_sb", [B, B, P], scope=scope)
        h2_hi, h2_lo = sb("h2_hi", [P, KC, N], F32R), sb("h2_lo", [P, KC, N], F32R)
        silu1, hid32 = sb("silu1", [P, 2, N]), sb("hid32", [P, 2, N])
        hid_hi, hid_lo = sb("hid_hi", [P, 2, N], F32R), sb("hid_lo", [P, 2, N], F32R)

        pa, pb, pc, pstate = bank("pa"), bank("pb"), bank("pc"), bank("pstate")
        pu1, pu3, pacc0, pacc1 = bank("pu1"), bank("pu3"), bank("pacc0"), bank("pacc1")
        pvg, po, py, pw = (pb, pc), (pa, pb), (pc, pb), (pa, pc)
        pacc, pffn = (pacc0, pacc1), (pu1, pu3, pacc0, pacc1)

        in_x0, in_xr, in_c, in_cst, in_mod1, in_mod2, in_wqkvg, in_wo, in_w2, in_cos, in_sin, in_gn, in_sel = (
            sem("in_" + n) for n in "x0 xr c cst mod1 mod2 wqkvg wo w2 cos sin gn sel".split())
        in_w13 = [sem(f"in_w13_{i}") for i in range(PIECES)]
        a_sc, a_gn, a_wqkvg, d_wqkvg, a_wo, d_wo_lo, a_w13, d_w13 = (
            sem(n) for n in "a_sc a_gn a_wqkvg d_wqkvg a_wo d_wo_lo a_w13 d_w13".split())
        t_cols1, t_cols2, t_rows, t_gates, d_cols1, d_cols2, d_rows, a_gates = (
            sem(n) for n in "t_cols1 t_cols2 t_rows t_gates d_cols1 d_cols2 d_rows a_gates".split())
        d_st1, d_mv1, p_ve1, p_rs1, p_mhalf, p_zero = (
            sem(n) for n in "d_st1 d_mv1 p_ve1 p_rs1 p_mhalf p_zero".split())
        p_fly, a_had, a_fly, d_fly, t_had, a_w2, d_w2 = (
            sem(n) for n in "p_fly a_had a_fly d_fly t_had a_w2 d_w2".split())
        d_cur, d_cur1, d_cur2, d_xn1, d_qb, a_qb, a_k, p_k = (
            sem(n, 1) for n in "d_cur d_cur1 d_cur2 d_xn1 d_qb a_qb a_k p_k".split())
        t_xn1, d_h1, a_h1, d_h1lo, t_qkt, a_qkt, d_qkt = (
            sem(n, 2) for n in "t_xn1 d_h1 a_h1 d_h1lo t_qkt a_qkt d_qkt".split())
        t_qk, t_vg, d_rope, p_rope, a_vg, d_vlo, p_gg = (
            sem(n, TILES) for n in "t_qk t_vg d_rope p_rope a_vg d_vlo p_gg".split())
        t_s, d_p, a_p, p_p, t_o, a_sq, d_y0, d_ss = (
            sem(n, TILES) for n in "t_s d_p a_p p_p t_o a_sq d_y0 d_ss".split())
        t_kv, d_s, a_s, p_s = (sem(n, TILES - 1) for n in "t_kv d_s a_s p_s".split())
        t_yt, a_yt, d_yt, t_wo, d_wo, d_x1, d_st2, d_mv2, p_ve2, p_rs2, d_xn2, t_xn2, d_h2, a_h2, d_h2lo, p_vo, p_rso, d_y = (
            sem(n, 2) for n in
            "t_yt a_yt d_yt t_wo d_wo d_x1 d_st2 d_mv2 p_ve2 p_rs2 d_xn2 t_xn2 d_h2 a_h2 d_h2lo p_vo p_rso d_y".split())
        t_u1, t_u3, a_silu, d_hid, a_hid, p_hid, t_d = (
            sem(n, HB) for n in "t_u1 t_u3 a_silu d_hid a_hid p_hid t_d".split())
        d_fin, d_out, stored = sem("d_fin", 2), sem("d_out", 2), sem("stored", 16)

        def run(engine, step):
            for kind, k in FIRST:
                step(kind, k, 0, None)
            with engine.Fori(1, B) as b:
                for kind, k in STEADY:
                    step(kind, k, b, b - 1)
            for kind, k in LAST:
                step(kind, k, None, B - 1)

        block = ctx.enter_context(nc.Block())

        @block.sync
        def _(sp):
            sp.dma_start(c_sb[:], c_t).then_inc(in_c.sem, 16)
            sp.dma_start(xres[:, 0], x[0].rearrange("(t p) d -> p t d", p=P)).then_inc(in_x0.sem, 16)
            sp.dma_start(wmod_sb[:, :, 0:2 * D], wmod[:, :, 0:2 * D]).then_inc(in_mod1.sem, 16)
            sp.dma_start(cst[:], consts).then_inc(in_cst.sem, 16)
            sp.dma_start(stage_qkvg[:], w_qkvg).then_inc(in_wqkvg.sem, 16)
            sp.dma_start(cos_sb[:], cos).then_inc(in_cos.sem, 16)
            sp.dma_start(sin_sb[:], sin).then_inc(in_sin.sem, 16)
            sp.dma_start(gnorm_in[:], gnorm).then_inc(in_gn.sem, 16)
            sp.dma_start(wmod_sb[:, :, 2 * D:6 * D], wmod[:, :, 2 * D:6 * D]).then_inc(in_mod2.sem, 16)
            sp.dma_start(sel_sb[:], select).then_inc(in_sel.sem, 16)
            sp.dma_start(fly0[:], w2).then_inc(in_w2.sem, 16)
            sp.dma_start(stage_wo[:], w_o).then_inc(in_wo.sem, 16)
            for i in range(PIECES):
                if i == 2:
                    sp.dma_start(xres[:, 1:B], x[1:B].rearrange("b (t p) d -> p (b t) d", p=P)
                                 ).then_inc(in_xr.sem, 16)
                if i >= 2:
                    sp.wait_ge(d_w13.sem, i - 1)
                sp.dma_start(stage_13[:, i % 2], w13[i]).then_inc(in_w13[i].sem, 16)

            def store(f):
                sp.wait_ge(d_out.sem, d_out.after(f, 2))
                sp.dma_start(out[f].rearrange("(t p) d -> p t d", p=P), xres[:, f]).then_inc(stored.sem, 16)

            with sp.Fori(1, B) as b:
                store(b - 1)
            store(B - 1)
            sp.wait_ge(stored.sem, stored.after(B, 0))

        @block.tensor
        def _(pe):
            def three(ps, parts, start=True, stop=True):
                ops = [(a, c) for (ah, al), (ch, cl) in parts for a, c in ((ah, ch), (ah, cl), (al, ch))]
                for n, (a, c) in enumerate(ops):
                    mm = pe.matmul(ps, a, c, start=start and n == 0, stop=stop and n == len(ops) - 1,
                                   skip_group_check=True)
                return mm

            def columns(parts, at, done):
                for part in parts:
                    for h in range(KC):
                        col = part * D + h * P
                        for kc in range(KC):
                            mm = pe.matmul(pu1[:, at:at + B], wmod_sb[:, kc, col:col + P], sc_sb[:, kc, :],
                                           start=(kc == 0), stop=(kc == KC - 1))
                        at += B
                mm.then_inc(done.sem, 1)

            def step(kind, k, b, f):
                first = b == 0 if isinstance(b, int) else False
                if kind == "M":
                    pe.wait_ge(in_mod1.sem, 16)
                    pe.wait_ge(a_sc.sem, 1)
                    columns((SA, CA), 0, t_cols1)
                elif kind == "G" and k == 0:
                    pe.wait_ge(in_mod2.sem, 16)
                    pe.wait_ge(in_sel.sem, 16)
                    pe.wait_ge(d_cols1.sem, 1)
                    columns((SB, CB), 2 * KC * B, t_cols2)
                    for n, part in enumerate((GA, GB)):
                        for kc in range(KC):
                            mm = pe.matmul(pu3[0:B, n * D:(n + 1) * D], sc_sb[:, kc, :],
                                           wmod_sb[:, kc, part * D:(part + 1) * D],
                                           start=(kc == 0), stop=(kc == KC - 1))
                    mm.then_inc(t_rows.sem, 1)
                elif kind == "G":
                    pe.wait_ge(d_rows.sem, 4)
                    for n in range(B):
                        pe.matmul(pffn[n][:, :], sel_sb[:, n, :], gate_row,
                                  start=True, stop=True).then_inc(t_gates.sem, 1)
                elif kind == "T":
                    if first:
                        pe.wait_ge(in_cst.sem, 16)
                    pe.wait_ge(d_xn1.sem, d_xn1.after(b, 1))
                    for kc in range(KC):
                        for t in range(TILES):
                            mm = pe.transpose((pa, pb)[kc][:, t * P:(t + 1) * P],
                                              xn[:, t, kc * P:(kc + 1) * P], ident)
                        mm.then_inc(t_xn1.sem, 1)
                elif kind == "P":
                    if k == 0:
                        pe.wait_ge(d_h1lo.sem, d_h1lo.after(b, KC))
                        if first:
                            pe.wait_ge(d_wqkvg.sem, 1)
                    else:
                        pe.wait_ge(d_rope.sem, d_rope.after(b, k))
                    tok = slice(k * P, (k + 1) * P)
                    three(pa[:, 0:QK], [((h1_hi[:, kc, tok], h1_lo[:, kc, tok]),
                                         (wqkvg_hi[:, kc, 0:QK], wqkvg_lo[:, kc, 0:QK])) for kc in range(KC)]
                          ).then_inc(t_qk.sem, 1)
                    if k >= 2:
                        pe.wait_ge(d_vlo.sem, d_vlo.after(b, k - 1))
                    three(pvg[k % 2][:, :], [((h1_hi[:, kc, tok], h1_lo[:, kc, tok]),
                                              (wqkvg_hi[:, kc, QK:QK + VG], wqkvg_lo[:, kc, QK:QK + VG]))
                                             for kc in range(KC)]).then_inc(t_vg.sem, 1)
                elif kind == "Q":
                    pe.wait_ge(p_rope.sem, p_rope.after(b, TILES))
                    for t in range(TILES):
                        mm = pe.transpose(pa[:, t * P:(t + 1) * P], qk[:, t, 0:P], ident)
                    mm.then_inc(t_qkt.sem, 1)
                    pe.wait_ge(d_vlo.sem, d_vlo.after(b, TILES - 1))
                    for t in range(TILES):
                        mm = pe.transpose(pb[:, t * P:(t + 1) * P], qk[:, t, P:2 * P], ident)
                    mm.then_inc(t_qkt.sem, 1)
                elif kind == "S":
                    if k == 0:
                        pe.wait_ge(d_qb.sem, d_qb.after(b, 1))
                        pe.wait_ge(a_qb.sem, a_qb.after(b, 1))
                    else:
                        pe.wait_ge(d_p.sem, d_p.after(b, k))
                    three(pc[:, :], [((kt_hi[:, k], kt_lo[:, k]), (qb_hi[:, k], qb_lo[:, k]))]
                          ).then_inc(t_s.sem, 1)
                elif kind == "K":
                    if k == 0:
                        pe.wait_ge(p_k.sem, p_k.after(b, 1))
                    else:
                        pe.wait_ge(d_s.sem, d_s.after(b, k))
                    three(pstate[:, 0:HEADS * DV], [((k_hi[:, k], k_lo[:, k]), (v_hi[:, k], v_lo[:, k]))],
                          start=(k == 0)).then_inc(t_kv.sem, 1)
                elif kind == "O":
                    if k >= 2:
                        pe.wait_ge(d_y0.sem, d_y0.after(b, k - 1))
                    if k:
                        pe.wait_ge(p_s.sem, p_s.after(b, k))
                        three(po[k % 2][:, 0:D], [((qt_hi[:, k], qt_lo[:, k]),
                                                   (s_hi[:, (k - 1) % 2], s_lo[:, (k - 1) % 2]))], stop=False)
                    pe.wait_ge(p_p.sem, p_p.after(b, k + 1))
                    for h in range(HEADS):
                        cols = slice(h * DV, (h + 1) * DV)
                        mm = three(po[k % 2][:, cols], [((p_hi[:, k % 2, h], p_lo[:, k % 2, h]),
                                                         (v_hi[:, k, cols], v_lo[:, k, cols]))],
                                   start=(k == 0 and h == 0), stop=(h == HEADS - 1))
                    mm.then_inc(t_o.sem, 1)
                elif kind == "Y":
                    pe.wait_ge(d_y.sem, d_y.after(b, k + 1))
                    for kc in range(KC):
                        for j in range(2):
                            mm = pe.transpose(py[k][:, (2 * kc + j) * P:(2 * kc + j + 1) * P],
                                              xn[:, 2 * k + j, kc * P:(kc + 1) * P], ident)
                    mm.then_inc(t_yt.sem, 1)
                elif kind == "W":
                    pe.wait_ge(d_yt.sem, d_yt.after(b, k + 1))
                    if k == 0:
                        pe.wait_ge(d_y0.sem, d_y0.after(b, 3))
                        if first:
                            pe.wait_ge(d_wo_lo.sem, 1)
                    for j in range(2):
                        tok = slice((2 * k + j) * P, (2 * k + j + 1) * P)
                        mm = three(pw[k][:, j * D:(j + 1) * D],
                                   [((h1_hi[:, kc, tok], h1_lo[:, kc, tok]), (wo_hi[:, kc], wo_lo[:, kc]))
                                    for kc in range(KC)])
                    mm.then_inc(t_wo.sem, 1)
                elif kind == "L":
                    pe.wait_ge(d_xn2.sem, d_xn2.after(b, 2))
                    for kc in range(KC):
                        for t in range(TILES):
                            mm = pe.transpose((pb, pa)[kc][:, t * P:(t + 1) * P],
                                              xn[:, t, kc * P:(kc + 1) * P], ident)
                        mm.then_inc(t_xn2.sem, 1)
                elif kind == "H":
                    pe.wait_ge(a_gates.sem, B)
                    pe.wait_ge(d_fly.sem, 1)
                    for n, ps in enumerate(pffn):
                        pe.matmul(ps[:, :], had_r[:], w2_hi[:, 2 * n:2 * n + 2, :], start=True, stop=False)
                        pe.matmul(ps[:, :], had_r[:], w2_lo[:, 2 * n:2 * n + 2, :], start=False, stop=True
                                  ).then_inc(t_had.sem, 1)
                elif kind == "U":
                    if k == 0:
                        pe.wait_ge(d_h2lo.sem, d_h2lo.after(f, KC))
                        pe.wait_ge(d_w2.sem, len(pffn))
                        pe.wait_ge(d_w13.sem, PIECES)
                    piece, col = divmod(k * P, PW)
                    for w, ps, read, done in ((0, pu1, a_silu, t_u1), (1, pu3, d_hid, t_u3)):
                        if k:
                            pe.wait_ge(read.sem, read.after(f, k))
                        three(ps[:, :], [((w13_hi[:, piece, w, kc, col:col + P],
                                           w13_lo[:, piece, w, kc, col:col + P]),
                                          (h2_hi[:, kc], h2_lo[:, kc])) for kc in range(KC)]
                              ).then_inc(done.sem, 1)
                elif kind == "D":
                    if k == 0 and isinstance(f, int):
                        pe.wait_ge(d_fin.sem, d_fin.after(f, 0))
                    pe.wait_ge(p_hid.sem, p_hid.after(f, k + 1))
                    for t in range(TILES):
                        tok = slice(t * P, (t + 1) * P)
                        mm = three(pacc[t // 2][:, t % 2 * D:(t % 2 + 1) * D],
                                   [((hid_hi[:, k % 2, tok], hid_lo[:, k % 2, tok]), (w2_hi[:, k], w2_lo[:, k]))],
                                   start=(k == 0 and t % 2 == 0), stop=(k == HB - 1))
                    mm.then_inc(t_d.sem, 1)

            run(pe, step)

        @block.vector
        def _(dve):
            def step(kind, k, b, f):
                first = b == 0 if isinstance(b, int) else False
                if kind == "R":
                    dve.wait_ge((in_xr if k else in_x0).sem, 16)
                    if k:
                        dve.wait_ge(d_mv1.sem, k)
                    for t in range(TILES):
                        ins = dve.bn_stats(stats1[:, t, :], xres[:, k, t])
                    ins.then_inc(d_st1.sem, 1)
                    dve.wait_ge(d_st1.sem, k + 1)
                    for t in range(TILES):
                        ins = dve.bn_aggr(mv1[:, k, t], stats1[:, t, :])
                    ins.then_inc(d_mv1.sem, 1)
                elif kind == "G" and k == 0:
                    dve.wait_ge(t_cols2.sem, 1)
                    for n, add in ((2, 0.0), (3, 1.0)):
                        ins = dve.tensor_scalar(mod_cols[:, :, n, :], pu1[:, n * KC * B:(n + 1) * KC * B].rearrange(
                            "p (h b) -> p b h", b=B), add, None, ALU.add)
                    ins.then_inc(d_cols2.sem, 1)
                    dve.wait_ge(t_rows.sem, 1)
                    dve.tensor_scalar(gate_row, pu3[0:B, :], 0.0, 2.0, ALU.is_ge, ALU.mult
                                      ).then_inc(d_rows.sem, 1)
                    dve.wait_ge(d_rows.sem, 1)
                    dve.scalar_tensor_tensor(out=gate_size, in0=gate_row, scalar=-1.0, in1=pu3[0:B, :],
                                             op0=ALU.add, op1=ALU.mult).then_inc(d_rows.sem, 1)
                    dve.wait_ge(d_rows.sem, 2)
                    dve.tensor_scalar(gate_size, gate_size, MIN_GATE, None, ALU.max).then_inc(d_rows.sem, 1)
                    dve.wait_ge(d_rows.sem, 3)
                    dve.scalar_tensor_tensor(out=gate_row, in0=gate_row, scalar=-1.0, in1=gate_size,
                                             op0=ALU.add, op1=ALU.mult).then_inc(d_rows.sem, 1)
                elif kind == "X" and k == 0:
                    dve.wait_ge(a_wqkvg.sem, 1)
                    dve.tensor_tensor(wqkvg_lo[:], stage_qkvg[:], wqkvg_hi[:].bitcast(F32), ALU.subtract
                                      ).then_inc(d_wqkvg.sem, 1)
                elif kind == "X":
                    if k == 1:
                        dve.wait_ge(a_wo.sem, 1)
                        dve.tensor_tensor(wo_lo[:], stage_wo[:], wo_hi[:].bitcast(F32), ALU.subtract
                                          ).then_inc(d_wo_lo.sem, 1)
                    dve.wait_ge(a_w13.sem, k)
                    dve.tensor_tensor(w13_lo[:, k - 1], stage_13[:, (k - 1) % 2], w13_hi[:, k - 1].bitcast(F32),
                                      ALU.subtract).then_inc(d_w13.sem, 1)
                elif kind == "V":
                    dve.wait_ge(a_fly.sem, 1)
                    dve.tensor_tensor(w2_lo[:], fly1[:], w2_hi[:].bitcast(F32), ALU.subtract
                                      ).then_inc(d_fly.sem, 1)
                elif kind == "H":
                    for n, ps in enumerate(pffn):
                        dve.wait_ge(a_w2.sem, n + 1)
                        dve.scalar_tensor_tensor(out=w2_lo[:, 2 * n:2 * n + 2, :], in0=ps[:, :].rearrange(
                            "p (n d) -> p n d", n=2), scalar=HID ** -0.5,
                            in1=w2_hi[:, 2 * n:2 * n + 2, :].bitcast(F32), op0=ALU.mult, op1=ALU.subtract
                            ).then_inc(d_w2.sem, 1)
                elif kind == "T":
                    dve.wait_ge(p_rs1.sem, 1 if first else B)
                    if not first:
                        dve.wait_ge(d_mv1.sem, B)
                    dve.tensor_copy(rs_cur[:], rs1[:, b])
                    dve.tensor_copy(mv_cur[:], mv1[:, b]).then_inc(d_cur.sem, 1)
                    dve.wait_ge(d_cur.sem, d_cur.after(b, 1))
                    for t in range(TILES):
                        ins = dve.tensor_scalar(xn[:, t], xres[:, b, t], mv_cur[:, t, 0:1], rs_cur[:, t:t + 1],
                                                ALU.subtract, ALU.mult)
                    ins.then_inc(d_xn1.sem, 1)
                    if first:
                        dve.wait_ge(t_cols1.sem, 1)
                        for n, add in ((0, 0.0), (1, 1.0)):
                            ins = dve.tensor_scalar(mod_cols[:, :, n, :], pu1[:, n * KC * B:(n + 1) * KC * B
                                                                              ].rearrange("p (h b) -> p b h", b=B),
                                                    add, None, ALU.add)
                        ins.then_inc(d_cols1.sem, 1)
                        dve.wait_ge(d_cols1.sem, 1)
                    dve.tensor_copy(mod_cur[:, 0:2], mod_cols[:, b, 0:2]).then_inc(d_cur1.sem, 1)
                    dve.wait_ge(d_cur1.sem, d_cur1.after(b, 1))
                    for kc in range(KC):
                        dve.wait_ge(t_xn1.sem, t_xn1.after(b, kc + 1))
                        dve.tensor_scalar(h32[:, kc], (pa, pb)[kc][:, :], mod_cur[:, 1, kc:kc + 1],
                                          mod_cur[:, 0, kc:kc + 1], ALU.mult, ALU.add).then_inc(d_h1.sem, 1)
                    for kc in range(KC):
                        dve.wait_ge(a_h1.sem, a_h1.after(b, kc + 1))
                        dve.tensor_tensor(h1_lo[:, kc], h32[:, kc], h1_hi[:, kc].bitcast(F32), ALU.subtract
                                          ).then_inc(d_h1lo.sem, 1)
                elif kind == "P":
                    if first and k == 0:
                        dve.wait_ge(in_cos.sem, 16)
                        dve.wait_ge(in_sin.sem, 16)
                    dve.wait_ge(t_qk.sem, t_qk.after(b, k + 1))
                    if k >= 2 or not first:
                        dve.wait_ge(p_rope.sem, p_rope.after(b, k - 1))
                    dve.tensor_tensor(rope_a[:, k % 2], pa[:, 0:QK], cos_sb[:, k], ALU.mult)
                    halves = [t.rearrange("p (g s e) -> p g s e", s=2, e=DK // 2)
                              for t in (rope_b[:, k % 2], pa[:, 0:QK], sin_sb[:, k])]
                    for s in range(2):
                        ins = dve.tensor_tensor(halves[0][:, :, 1 - s], halves[1][:, :, s], halves[2][:, :, s],
                                                ALU.mult)
                    ins.then_inc(d_rope.sem, 1)
                    dve.wait_ge(a_vg.sem, a_vg.after(b, k + 1))
                    dve.tensor_tensor(v_lo[:, k], pvg[k % 2][:, 0:D], v_hi[:, k].bitcast(F32), ALU.subtract
                                      ).then_inc(d_vlo.sem, 1)
                elif kind == "Q":
                    for n, (ps, hi, lo) in enumerate(((pa, qt_hi, qt_lo), (pb, kt_hi, kt_lo))):
                        dve.wait_ge(a_qkt.sem, a_qkt.after(b, n + 1))
                        dve.tensor_tensor(lo[:], ps[:, :].rearrange("p (t i) -> p t i", t=TILES),
                                          hi[:].bitcast(F32), ALU.subtract).then_inc(d_qkt.sem, 1)
                    if first:
                        dve.wait_ge(p_zero.sem, 2)
                    for h in range(HEADS):
                        rows = slice(h * DK, (h + 1) * DK)
                        ins = dve.tensor_copy(qb_hi[rows, :, h, :], qt_hi[rows].bitcast(F32))
                    ins.then_inc(d_qb.sem, 1)
                elif kind == "S":
                    if k >= 2:
                        dve.wait_ge(p_p.sem, p_p.after(b, k - 1))
                    dve.wait_ge(t_s.sem, t_s.after(b, k + 1))
                    dve.tensor_tensor(p32[:, k % 2], pc[:, :].rearrange("p (h i) -> p h i", h=HEADS),
                                      causal.unsqueeze(1).to_broadcast([P, HEADS, P]), ALU.mult
                                      ).then_inc(d_p.sem, 1)
                elif kind == "K":
                    dve.wait_ge(t_kv.sem, t_kv.after(b, k + 1))
                    if k:
                        dve.wait_ge(p_s.sem, p_s.after(b, k))
                    dve.tensor_tensor(s32[:], pstate[:, 0:HEADS * DV], blocks, ALU.mult).then_inc(d_s.sem, 1)
                elif kind == "O":
                    dve.wait_ge(a_sq.sem, a_sq.after(b, k + 1))
                    dve.wait_ge(p_gg.sem, p_gg.after(b, k + 1))
                    dve.tensor_tensor(xn[:, k], po[k % 2][:, 0:D], gg[:, k], ALU.mult).then_inc(d_y0.sem, 1)
                    dve.reduce_sum(ss[:, k], sq[:, k % 2].rearrange("p (h v) -> p h v", h=HEADS), AX.X
                                   ).then_inc(d_ss.sem, 1)
                elif kind == "N":
                    dve.wait_ge(p_rso.sem, p_rso.after(b, k + 1))
                    pair = slice(2 * k, 2 * k + 2)
                    y = xn[:, pair].rearrange("p t (h v) -> p (t h) v", h=HEADS)
                    dve.wait_ge(d_y0.sem, d_y0.after(b, 2 * k + 2))
                    dve.tensor_tensor(y, y, rso[:, pair].rearrange("p t h -> p (t h)").unsqueeze(2).to_broadcast(
                        [P, 2 * HEADS, DV]), ALU.mult).then_inc(d_y.sem, 1)
                elif kind == "Y":
                    dve.wait_ge(a_yt.sem, a_yt.after(b, k + 1))
                    tok = slice(2 * k * P, (2 * k + 2) * P)
                    dve.tensor_tensor(h1_lo[:, :, tok], py[k][:, :].rearrange("p (k n) -> p k n", k=KC),
                                      h1_hi[:, :, tok].bitcast(F32), ALU.subtract).then_inc(d_yt.sem, 1)
                elif kind == "W":
                    dve.wait_ge(t_wo.sem, t_wo.after(b, k + 1))
                    if first and k == 0:
                        dve.wait_ge(a_gates.sem, B)
                    pair = slice(2 * k, 2 * k + 2)
                    dve.tensor_tensor(tmp[:], pw[k][:, :].rearrange("p (t d) -> p t d", t=2),
                                      gates[:, b, 0].unsqueeze(1).to_broadcast([P, 2, D]), ALU.mult
                                      ).then_inc(d_wo.sem, 1)
                    dve.wait_ge(d_wo.sem, d_wo.after(b, k + 1))
                    dve.tensor_tensor(x1[:, pair], xres[:, b, pair], tmp[:], ALU.add).then_inc(d_x1.sem, 1)
                    dve.wait_ge(d_x1.sem, d_x1.after(b, k + 1))
                    for t in (2 * k, 2 * k + 1):
                        ins = dve.bn_stats(stats[:, t, :], x1[:, t])
                    ins.then_inc(d_st2.sem, 1)
                    dve.wait_ge(d_st2.sem, d_st2.after(b, k + 1))
                    dve.tensor_scalar(xres[:, b, pair], x1[:, pair], 1.0, None, ALU.mult)
                    for t in (2 * k, 2 * k + 1):
                        ins = dve.bn_aggr(mv2[:, t], stats[:, t, :])
                    ins.then_inc(d_mv2.sem, 1)
                elif kind == "L":
                    if first:
                        dve.wait_ge(d_cols2.sem, 1)
                    dve.tensor_copy(mod_cur[:, 2:4], mod_cols[:, b, 2:4]).then_inc(d_cur2.sem, 1)
                    for n in range(2):
                        dve.wait_ge(p_rs2.sem, p_rs2.after(b, n + 1))
                        for t in (2 * n, 2 * n + 1):
                            ins = dve.tensor_scalar(xn[:, t], x1[:, t], mv2[:, t, 0:1], rs2[:, t:t + 1],
                                                    ALU.subtract, ALU.mult)
                        ins.then_inc(d_xn2.sem, 1)
                    dve.wait_ge(d_cur2.sem, d_cur2.after(b, 1))
                    for kc in range(KC):
                        dve.wait_ge(t_xn2.sem, t_xn2.after(b, kc + 1))
                        dve.tensor_scalar(h32[:, kc], (pb, pa)[kc][:, :], mod_cur[:, 3, kc:kc + 1],
                                          mod_cur[:, 2, kc:kc + 1], ALU.mult, ALU.add).then_inc(d_h2.sem, 1)
                    for kc in range(KC):
                        dve.wait_ge(a_h2.sem, a_h2.after(b, kc + 1))
                        dve.tensor_tensor(h2_lo[:, kc], h32[:, kc], h2_hi[:, kc].bitcast(F32), ALU.subtract
                                          ).then_inc(d_h2lo.sem, 1)
                elif kind == "U":
                    dve.wait_ge(t_u3.sem, t_u3.after(f, k + 1))
                    dve.wait_ge(a_silu.sem, a_silu.after(f, k + 1))
                    if k >= 2:
                        dve.wait_ge(p_hid.sem, p_hid.after(f, k - 1))
                    dve.tensor_tensor(hid32[:, k % 2], silu1[:, k % 2], pu3[:, :], ALU.mult
                                      ).then_inc(d_hid.sem, 1)
                elif kind == "F":
                    dve.wait_ge(t_d.sem, t_d.after(f, HB))
                    for n in range(2):
                        pair = slice(2 * n, 2 * n + 2)
                        if n:
                            dve.wait_ge(d_out.sem, d_out.after(f, n))
                        dve.tensor_tensor(tmp[:], pacc[n][:, :].rearrange("p (t d) -> p t d", t=2),
                                          gates[:, f, 1].unsqueeze(1).to_broadcast([P, 2, D]), ALU.mult
                                          ).then_inc(d_fin.sem, 1)
                        dve.wait_ge(d_fin.sem, d_fin.after(f, n + 1))
                        dve.tensor_tensor(xres[:, f, pair], xres[:, f, pair], tmp[:], ALU.add
                                          ).then_inc(d_out.sem, 1)

            run(dve, step)

        @block.scalar
        def _(act):
            act.wait_ge(in_c.sem, 16)
            act.activation(sc_sb[:], c_sb[:], ACT.Silu).then_inc(a_sc.sem, 1)
            act.wait_ge(in_gn.sem, 16)
            act.activation(gnorm_sb[:], gnorm_in[:], ACT.Copy, scale=DV ** 0.5).then_inc(a_gn.sem, 1)

            def step(kind, k, b, f):
                first = b == 0 if isinstance(b, int) else False
                if kind == "X" and k == 0:
                    act.wait_ge(in_wqkvg.sem, 16)
                    act.activation(wqkvg_hi[:], stage_qkvg[:], ACT.Copy).then_inc(a_wqkvg.sem, 1)
                    act.wait_ge(in_cst.sem, 16)
                    act.activation(had_r[:], hadamard, ACT.Copy).then_inc(a_had.sem, 1)
                elif kind == "X":
                    if k == 1:
                        act.wait_ge(in_wo.sem, 16)
                        act.activation(wo_hi[:], stage_wo[:], ACT.Copy).then_inc(a_wo.sem, 1)
                    act.wait_ge(in_w13[k - 1].sem, 16)
                    act.activation(w13_hi[:, k - 1], stage_13[:, (k - 1) % 2], ACT.Copy).then_inc(a_w13.sem, 1)
                elif kind == "G" and k == 1:
                    for n in range(B):
                        act.wait_ge(t_gates.sem, n + 1)
                        act.activation(gates[:, n].rearrange("p g d -> p (g d)"), pffn[n][:, :], ACT.Copy
                                       ).then_inc(a_gates.sem, 1)
                elif kind == "V":
                    act.wait_ge(p_fly.sem, 3)
                    act.activation(w2_hi[:], fly1[:], ACT.Copy).then_inc(a_fly.sem, 1)
                elif kind == "H":
                    act.wait_ge(t_had.sem, len(pffn))
                    for n, ps in enumerate(pffn):
                        act.activation(w2_hi[:, 2 * n:2 * n + 2, :], ps[:, :].rearrange("p (n d) -> p n d", n=2),
                                       ACT.Copy, scale=HID ** -0.5).then_inc(a_w2.sem, 1)
                elif kind == "T":
                    for kc in range(KC):
                        act.wait_ge(d_h1.sem, d_h1.after(b, kc + 1))
                        act.activation(h1_hi[:, kc], h32[:, kc], ACT.Copy).then_inc(a_h1.sem, 1)
                elif kind == "P":
                    act.wait_ge(t_vg.sem, t_vg.after(b, k + 1))
                    act.activation(v_hi[:, k], pvg[k % 2][:, 0:D], ACT.Copy)
                    if k >= 2:
                        act.wait_ge(p_gg.sem, p_gg.after(b, k - 1))
                    act.activation(g32[:, k % 2], pvg[k % 2][:, D:2 * D], ACT.Silu).then_inc(a_vg.sem, 1)
                elif kind == "Q":
                    for n, (ps, hi) in enumerate(((pa, qt_hi), (pb, kt_hi))):
                        act.wait_ge(t_qkt.sem, t_qkt.after(b, n + 1))
                        act.activation(hi[:], ps[:, :].rearrange("p (t i) -> p t i", t=TILES), ACT.Copy
                                       ).then_inc(a_qkt.sem, 1)
                    act.wait_ge(p_rope.sem, p_rope.after(b, TILES))
                    act.activation(k_hi[:], qk[:, :, P:2 * P], ACT.Copy).then_inc(a_k.sem, 1)
                    if first:
                        act.wait_ge(p_zero.sem, 2)
                    act.wait_ge(d_qkt.sem, d_qkt.after(b, 1))
                    for h in range(HEADS):
                        rows = slice(h * DK, (h + 1) * DK)
                        ins = act.activation(qb_lo[rows, :, h, :], qt_lo[rows].bitcast(F32), ACT.Copy)
                    ins.then_inc(a_qb.sem, 1)
                elif kind == "S":
                    if k >= 2:
                        act.wait_ge(t_o.sem, t_o.after(b, k - 1))
                    act.wait_ge(d_p.sem, d_p.after(b, k + 1))
                    act.activation(p_hi[:, k % 2], p32[:, k % 2], ACT.Copy).then_inc(a_p.sem, 1)
                elif kind == "K":
                    if k >= 2:
                        act.wait_ge(t_o.sem, t_o.after(b, k))
                    act.wait_ge(d_s.sem, d_s.after(b, k + 1))
                    act.activation(s_hi[:, k % 2], s32[:], ACT.Copy).then_inc(a_s.sem, 1)
                elif kind == "O":
                    act.wait_ge(t_o.sem, t_o.after(b, k + 1))
                    if k >= 2:
                        act.wait_ge(d_ss.sem, d_ss.after(b, k - 1))
                    act.activation(sq[:, k % 2], po[k % 2][:, 0:D], ACT.Square).then_inc(a_sq.sem, 1)
                elif kind == "Y":
                    act.wait_ge(t_yt.sem, t_yt.after(b, k + 1))
                    act.activation(h1_hi[:, :, 2 * k * P:(2 * k + 2) * P],
                                   py[k][:, :].rearrange("p (k n) -> p k n", k=KC), ACT.Copy).then_inc(a_yt.sem, 1)
                elif kind == "L":
                    for kc in range(KC):
                        act.wait_ge(d_h2.sem, d_h2.after(b, kc + 1))
                        act.activation(h2_hi[:, kc], h32[:, kc], ACT.Copy).then_inc(a_h2.sem, 1)
                elif kind == "U":
                    act.wait_ge(t_u1.sem, t_u1.after(f, k + 1))
                    if k >= 2:
                        act.wait_ge(d_hid.sem, d_hid.after(f, k - 1))
                    act.activation(silu1[:, k % 2], pu1[:, :], ACT.Silu).then_inc(a_silu.sem, 1)
                    act.wait_ge(d_hid.sem, d_hid.after(f, k + 1))
                    if k >= 2:
                        act.wait_ge(t_d.sem, t_d.after(f, k - 1))
                    act.activation(hid_hi[:, k % 2], hid32[:, k % 2], ACT.Copy).then_inc(a_hid.sem, 1)

            run(act, step)

        @block.gpsimd
        def _(pool):
            pool.memset(eps_ln[:], EPS).then_inc(p_mhalf.sem, 1)
            pool.memset(eps_rms[:], DV * EPS).then_inc(p_mhalf.sem, 1)
            pool.memset(mhalf[:], -0.5).then_inc(p_mhalf.sem, 1)

            def step(kind, k, b, f):
                first = b == 0 if isinstance(b, int) else False
                if kind == "R":
                    pool.wait_ge(p_mhalf.sem, 3)
                    pool.wait_ge(d_mv1.sem, k + 1)
                    pool.tensor_tensor(ve1[:, k], mv1[:, k, :, 1], eps_ln[:], ALU.add).then_inc(p_ve1.sem, 1)
                    pool.wait_ge(p_ve1.sem, k + 1)
                    pool.tensor_tensor(rs1[:, k], ve1[:, k], mhalf[:, 0:TILES], ALU.pow).then_inc(p_rs1.sem, 1)
                elif kind == "G" and k == 0:
                    pool.wait_ge(t_rows.sem, 1)
                    pool.wait_ge(d_wqkvg.sem, 1)
                    pool.memset(qb_hi[:].bitcast(F32), 0.0).then_inc(p_zero.sem, 1)
                    pool.memset(qb_lo[:].bitcast(F32), 0.0).then_inc(p_zero.sem, 1)
                elif kind == "J":
                    if k == 0:
                        pool.wait_ge(in_w2.sem, 16)
                    else:
                        pool.wait_ge(p_fly.sem, k)
                    src, dst = (t[:].rearrange("p (g s r) d -> p g s (r d)", s=2, r=2 ** k)
                                for t in ((fly0, fly1), (fly1, fly0))[k % 2])
                    pool.tensor_tensor(dst[:, :, 0], src[:, :, 0], src[:, :, 1], ALU.add)
                    pool.tensor_tensor(dst[:, :, 1], src[:, :, 0], src[:, :, 1], ALU.subtract
                                       ).then_inc(p_fly.sem, 1)
                elif kind == "P":
                    pool.wait_ge(d_rope.sem, d_rope.after(b, k + 1))
                    pool.tensor_tensor(qk[:, k], rope_a[:, k % 2], rope_b[:, k % 2], ALU.add
                                       ).then_inc(p_rope.sem, 1)
                    if first and k == 0:
                        pool.wait_ge(a_gn.sem, 1)
                    pool.wait_ge(a_vg.sem, a_vg.after(b, k + 1))
                    pool.tensor_tensor(gg[:, k].rearrange("p (h v) -> p h v", h=HEADS),
                                       g32[:, k % 2].rearrange("p (h v) -> p h v", h=HEADS),
                                       gnorm_sb[:].unsqueeze(1).to_broadcast([P, HEADS, DV]), ALU.mult
                                       ).then_inc(p_gg.sem, 1)
                elif kind == "Q":
                    pool.wait_ge(a_k.sem, a_k.after(b, 1))
                    pool.tensor_tensor(k_lo[:], qk[:, :, P:2 * P], k_hi[:].bitcast(F32), ALU.subtract
                                       ).then_inc(p_k.sem, 1)
                elif kind == "S":
                    pool.wait_ge(a_p.sem, a_p.after(b, k + 1))
                    pool.tensor_tensor(p_lo[:, k % 2], p32[:, k % 2], p_hi[:, k % 2].bitcast(F32), ALU.subtract
                                       ).then_inc(p_p.sem, 1)
                elif kind == "K":
                    pool.wait_ge(a_s.sem, a_s.after(b, k + 1))
                    pool.tensor_tensor(s_lo[:, k % 2], s32[:], s_hi[:, k % 2].bitcast(F32), ALU.subtract
                                       ).then_inc(p_s.sem, 1)
                elif kind == "N":
                    s2, v2, r2 = (t[:, 2 * k:2 * k + 2].rearrange("p t h -> p (t h)") for t in (ss, vo, rso))
                    pool.wait_ge(d_ss.sem, d_ss.after(b, 2 * k + 2))
                    pool.tensor_tensor(v2, s2, eps_rms[:], ALU.add).then_inc(p_vo.sem, 1)
                    pool.wait_ge(p_vo.sem, p_vo.after(b, k + 1))
                    pool.tensor_tensor(r2, v2, mhalf[:], ALU.pow).then_inc(p_rso.sem, 1)
                elif kind == "W":
                    pair = slice(2 * k, 2 * k + 2)
                    pool.wait_ge(d_mv2.sem, d_mv2.after(b, k + 1))
                    pool.tensor_tensor(ve2[:, pair], mv2[:, pair, 1], eps_ln[:, 0:2], ALU.add).then_inc(p_ve2.sem, 1)
                    pool.wait_ge(p_ve2.sem, p_ve2.after(b, k + 1))
                    pool.tensor_tensor(rs2[:, pair], ve2[:, pair], mhalf[:, 0:2], ALU.pow).then_inc(p_rs2.sem, 1)
                elif kind == "U":
                    pool.wait_ge(a_hid.sem, a_hid.after(f, k + 1))
                    pool.tensor_tensor(hid_lo[:, k % 2], hid32[:, k % 2], hid_hi[:, k % 2].bitcast(F32),
                                       ALU.subtract).then_inc(p_hid.sem, 1)

            run(pool, step)


def constants():
    i = np.arange(P)
    head = np.arange(QK) % P // DK
    consts = np.zeros((P, C_END), np.float32)
    consts[:, C_IDENT:C_IDENT + P] = np.eye(P)
    consts[:, C_CAUSAL:C_CAUSAL + P] = i[None, :] >= i[:, None]
    bits = np.array([[bin(r & c).count("1") for c in range(P)] for r in range(P)])
    consts[:, C_HADAMARD:C_HADAMARD + P] = 1 - 2 * (bits % 2)
    consts[:, C_BLOCKS:C_END] = i[:, None] // DK == np.arange(HEADS * DV)[None, :] // DV
    select = np.zeros((B, B, P), np.float32)
    for b in range(B):
        select[b, b] = 1
    inv_freq = (np.float32(1) / np.float32(10000) ** (np.arange(0, DK, 2, dtype=np.float32) / np.float32(DK)))
    angle = (np.arange(N, dtype=np.float32)[:, None] * inv_freq.astype(np.float32)).astype(np.float64)
    angle = angle[:, np.arange(QK) % (DK // 2)]
    gamma = 1.0 - 2.0 ** (-5.0 - head)
    is_q = np.arange(QK) < P
    power = np.arange(N)[:, None] * np.where(is_q, 1.0, -1.0)
    factor = gamma ** power * np.where(is_q, DK ** -0.5, 1.0)
    sign = np.where(np.arange(QK) % DK < DK // 2, 1.0, -1.0)
    tile = lambda a: np.ascontiguousarray(a.astype(np.float32).reshape(TILES, P, QK).transpose(1, 0, 2))
    return consts, select, tile(np.cos(angle) * factor), tile(np.sin(angle) * factor * sign)


def rows_to_partitions(w):
    return np.ascontiguousarray(w.reshape(-1, P, w.shape[1]).transpose(1, 0, 2))


def kernel(L0_attn_x, L0_attn_Wq, L0_attn_Wk, L0_attn_Wv, L0_attn_Wg, L0_attn_Wo, L0_attn_gnorm_w,
           L0_ffn_W1, L0_ffn_W2, L0_ffn_W3, L0_c, L0_wmod):
    import concourse.bacc as bacc
    from concourse.bass_utils import run_bass_kernel_spmd

    arr = np.asarray
    w_qkvg = rows_to_partitions(np.concatenate([arr(w) for w in (L0_attn_Wq, L0_attn_Wk, L0_attn_Wv, L0_attn_Wg)]).T)
    w13 = np.stack([rows_to_partitions(arr(w).T) for w in (L0_ffn_W1, L0_ffn_W3)])
    w13 = np.ascontiguousarray(w13.reshape(2, P, KC, PIECES, PW).transpose(3, 1, 0, 2, 4))
    consts, select, cos, sin = constants()
    arrays = {
        "x": arr(L0_attn_x),
        "c_t": rows_to_partitions(arr(L0_c).T),
        "w_qkvg": w_qkvg,
        "w_o": rows_to_partitions(arr(L0_attn_Wo).T),
        "gnorm": np.ascontiguousarray(np.broadcast_to(arr(L0_attn_gnorm_w), (P, DV))),
        "w13": w13,
        "w2": rows_to_partitions(arr(L0_ffn_W2).T),
        "wmod": rows_to_partitions(arr(L0_wmod)),
        "consts": consts, "select": select, "cos": cos, "sin": sin,
    }
    nc = bacc.Bacc("TRN2", target_bir_lowering=False, num_devices=1)
    args = [nc.dram_tensor(name, a.shape, mybir.dt.from_np(a.dtype), kind="ExternalInput").ap()
            for name, a in arrays.items()]
    args.append(nc.dram_tensor("out", (B, N, D), F32, kind="ExternalOutput").ap())
    adaln_block_kernel(nc, *args)
    return run_bass_kernel_spmd(nc, [arrays], core_ids=[0]).results[0]["out"]
```

```python
from contextlib import ExitStack

import numpy as np

import concourse.bass as bass
from concourse import mybir

P = 128
B, N, D = 4, 512, 256
HEADS, DK, DV = 4, 32, 64
HID = 1024
TILES = N // P
KC = D // P
QK = 2 * HEADS * DK
VG = 2 * HEADS * DV
HB = HID // P
PIECES = 4
PW = HID // PIECES
STAGES, PARTS = 3, 4
FLY_A, FLY_B = (0, 1), (2, 3)
EPS = 1e-5
MIN_GATE = 0.25
SA, CA, GA, SB, CB, GB = range(6)

F32 = mybir.dt.float32
F32R = mybir.dt.float32r
ALU = mybir.AluOpType
ACT = mybir.ActivationFunctionType
AX = mybir.AxisListType

C_IDENT, C_CAUSAL, C_HADAMARD, C_BLOCKS, C_END = 0, P, 2 * P, 3 * P, 3 * P + HEADS * DV


def steps(text):
    return [(name, int(k)) for name, k in (word.split(".") for word in text.split())]


FIRST = steps("stats.0 norm.0 norm.1 fly_b.0 mod.0 h1.0 h1lo.0 w_hi.0 h1.1 w_lo.0 mod.1 h1lo.1 fly_a.0 fly_a.1 qk.0 "
              "w_o.0 fly_b.1 fly_a.2 rows.0 zero.0 vg.0 qk.1 fly_b.2 fly_a.3 w_w13.0 vg.1 qk.2 w_w13.1 vg.2 qk.3 "
              "vg.3 fly_b.3 stats.1 ksplit.0 fly_b.4 qt.0 kt.0 qblk.0 stats.2 gates.0 score.0 fly_a.4 state.0 plo.0 "
              "score.1 state.1 fly_a.5 fly_b.5 score.2 plo.1 o.0 state.2 score.3 plo.2 o.1 plo.3 ss.0 ss.1 w_w13.2 "
              "o.2 o.3 rms.0 ss.2 ss.3 w_w13.3 yt.0 rms.1 fold.0 proj.0 yt.1 had.0 proj.1 norm2.0 norm2.1 h2.0 h2.1 "
              "h2lo.0 h2lo.1 stats.3")
STEADY = steps("norm.0 norm.1 up.0 h1.0 hid.0 h1lo.0 up.1 h1.1 qk.0 hid.1 h1lo.1 up.2 qk.1 vg.0 qk.2 vg.1 vg.2 qk.3 "
               "vg.3 ksplit.0 down.0 hid.2 qt.0 kt.0 qblk.0 up.3 down.1 score.0 state.0 plo.0 down.2 score.1 state.1 "
               "plo.1 o.0 hid.3 score.2 state.2 o.1 ss.0 plo.2 ss.1 up.4 score.3 plo.3 o.2 down.3 rms.0 hid.4 ss.2 "
               "o.3 ss.3 yt.0 up.5 rms.1 proj.0 down.4 yt.1 norm2.0 hid.5 up.6 hid.6 proj.1 up.7 norm2.1 hid.7 h2.0 "
               "down.5 h2.1 down.6 h2lo.0 down.7 h2lo.1 out.0 out.1")
LAST = steps("up.0 hid.0 up.1 hid.1 up.2 up.3 down.0 hid.2 hid.3 down.1 up.4 up.5 hid.4 down.2 down.3 hid.5 up.6 "
             "up.7 down.4 hid.6 hid.7 down.5 down.6 down.7 out.0 out.1")


class Signal:

    def __init__(self, sem, per, start=0):
        self.sem, self.per, self.start = sem, per, start

    def after(self, batch, k):
        return batch * self.per + (self.start + k)


def adaln_block_kernel(nc, x, c_t, w_qkvg, w_o, gnorm, w13, w2, wmod, consts, select, cos, sin, out):
    with ExitStack() as ctx:
        def sb(name, shape, dt=F32, scope=ctx):
            return scope.enter_context(nc.sbuf_tensor(name, shape, dt))

        def bank(name):
            return ctx.enter_context(nc.psum_tensor(name, [P, 512], F32))

        def sem(name, per=0, start=0):
            return Signal(ctx.enter_context(nc.semaphore(name)), per, start)

        xres = sb("xres", [P, B, TILES, D])
        mod_cols = sb("mod_cols", [P, B, 4, KC])
        gates = sb("gates", [P, B, 2, D])
        cst = sb("cst", [P, C_END])
        ident, causal = cst[:, C_IDENT:C_IDENT + P], cst[:, C_CAUSAL:C_CAUSAL + P]
        hadamard, blocks = cst[:, C_HADAMARD:C_HADAMARD + P], cst[:, C_BLOCKS:C_END]
        had_r = sb("had_r", [P, P], F32R)
        cos_sb, sin_sb = sb("cos_sb", [P, TILES, QK]), sb("sin_sb", [P, TILES, QK])
        gnorm_in, gnorm_sb = sb("gnorm_in", [P, DV]), sb("gnorm_sb", [P, DV])
        mhalf = sb("mhalf", [P, 2 * HEADS])
        eps_ln, eps_rms = sb("eps_ln", [P, TILES]), sb("eps_rms", [P, 2 * HEADS])
        c_sb, sc_sb = sb("c_sb", [P, KC, B]), sb("sc_sb", [P, KC, B])
        mv1 = sb("mv1", [P, B, TILES, 2])
        ve1, rs1 = sb("ve1", [P, B, TILES]), sb("rs1", [P, B, TILES])
        wqkvg_hi, wqkvg_lo = (sb("wqkvg_" + e, [P, KC, QK + VG], F32R) for e in ("hi", "lo"))
        wo_hi, wo_lo = (sb("wo_" + e, [P, KC, D], F32R) for e in ("hi", "lo"))
        w13_hi, w13_lo = (sb("w13_" + e, [P, PIECES, 2, KC, PW], F32R) for e in ("hi", "lo"))

        stats1, stats = sb("stats1", [P, TILES, 6]), sb("stats", [P, TILES, 6])
        mv_cur, rs_cur = sb("mv_cur", [P, TILES, 2]), sb("rs_cur", [P, TILES])
        mod_cur = sb("mod_cur", [P, 4, KC])
        mv2, ve2, rs2 = sb("mv2", [P, TILES, 2]), sb("ve2", [P, TILES]), sb("rs2", [P, TILES])
        xn = sb("xn", [P, TILES, D])
        h32 = sb("h32", [P, KC, N])
        p32 = h32[:, :, :].rearrange("p k (h i) -> p k h i", h=HEADS)
        h1_hi, h1_lo = sb("h1_hi", [P, KC, N], F32R), sb("h1_lo", [P, KC, N], F32R)
        rope_a, rope_b = sb("rope_a", [P, 2, QK]), sb("rope_b", [P, 2, QK])
        qk = sb("qk", [P, TILES, QK])
        x1 = qk
        k_hi, k_lo = sb("k_hi", [P, TILES, P], F32R), sb("k_lo", [P, TILES, P], F32R)
        v2 = sb("v2", [P, TILES, HEADS, 2, DV], F32R)
        v_hi, v_lo = v2[:, :, :, 0, :], v2[:, :, :, 1, :]
        gg = sb("gg", [P, TILES, D])
        qt_hi, qt_lo = sb("qt_hi", [P, TILES, P], F32R), sb("qt_lo", [P, TILES, P], F32R)
        kt_hi, kt_lo = sb("kt_hi", [P, TILES, P], F32R), sb("kt_lo", [P, TILES, P], F32R)
        p_hi, p_lo = sb("p_hi", [P, 2, HEADS, P], F32R), sb("p_lo", [P, 2, HEADS, P], F32R)
        s32 = sb("s32", [P, HEADS * DV])
        s_hi, s_lo = sb("s_hi", [P, 2, HEADS * DV], F32R), sb("s_lo", [P, 2, HEADS * DV], F32R)
        sq = sb("sq", [P, 2, D])
        ss, vo, rso = (sb(n, [P, TILES, HEADS]) for n in ("ss", "vo", "rso"))
        tmp = sb("tmp", [P, 2, D])
        branch = (tmp, sq)
        unused = sb("unused", [P, 2])

        gate_row = tmp[0:B].rearrange("b g d -> b (g d)")
        gate_size = sq[0:B].rearrange("b g d -> b (g d)")

        with ExitStack() as scope:
            fly0 = sb("fly0", [P, HB, D], scope=scope)
        w2_hi = sb("w2_hi", [P, HB, D], F32R)
        w2_lo = sb("w2_lo", [P, HB, D], F32R)
        with ExitStack() as scope:
            wmod_sb = sb("wmod_sb", [P, KC, 6 * D], scope=scope)
            stage_qkvg = sb("stage_qkvg", [P, KC, QK + VG], scope=scope)
        qb_hi = sb("qb_hi", [P, TILES, HEADS, P], F32R)
        qb_lo = sb("qb_lo", [P, TILES, HEADS, P], F32R)
        g32 = sb("g32", [P, 2, D])
        with ExitStack() as scope:
            fly1 = sb("fly1", [P, HB, D], scope=scope)
            stage_13 = sb("stage_13", [P, 2, 2, KC, PW], scope=scope)
            stage_wo = sb("stage_wo", [P, KC, D], scope=scope)
            sel_sb = sb("sel_sb", [B, B, P], scope=scope)
        h2_hi, h2_lo = sb("h2_hi", [P, KC, N], F32R), sb("h2_lo", [P, KC, N], F32R)
        silu1, hid32 = sb("silu1", [P, 2, N]), sb("hid32", [P, 2, N])
        hid_hi, hid_lo = sb("hid_hi", [P, 2, N], F32R), sb("hid_lo", [P, 2, N], F32R)

        pa, pb, pc, pstate = bank("pa"), bank("pb"), bank("pc"), bank("pstate")
        pu1, pu3, pacc0, pacc1 = bank("pu1"), bank("pu3"), bank("pacc0"), bank("pacc1")
        ph1, pvg, po, py, pw, ph2 = (pa, pb), (pc, pb), (pa, pb), (pc, pb), (pa, pc), (pb, pa)
        pacc, pffn = (pacc0, pacc1), (pu1, pu3, pacc0, pacc1)

        in_x0, in_xr, in_c, in_cst, in_mod1, in_mod2, in_wqkvg, in_wo, in_w2, in_cos, in_sin, in_gn, in_sel = (
            sem("in_" + n) for n in "x0 xr c cst mod1 mod2 wqkvg wo w2 cos sin gn sel".split())
        in_w13 = [sem(f"in_w13_{i}") for i in range(PIECES)]
        a_sc, a_gn, a_wqkvg, d_wqkvg, a_wo, d_wo_lo, a_w13, d_w13 = (
            sem(n) for n in "a_sc a_gn a_wqkvg d_wqkvg a_wo d_wo_lo a_w13 d_w13".split())
        t_cols1, t_cols2, t_rows, t_gates, d_cols1, d_cols2, d_rows, a_gates = (
            sem(n) for n in "t_cols1 t_cols2 t_rows t_gates d_cols1 d_cols2 d_rows a_gates".split())
        d_st1, d_mv1, p_ve1, p_rs1, p_mhalf, p_zero = (
            sem(n) for n in "d_st1 d_mv1 p_ve1 p_rs1 p_mhalf p_zero".split())
        p_fly, a_had, a_fly, d_flya, d_fly, t_had, a_w2, d_w2 = (
            sem(n) for n in "p_fly a_had a_fly d_flya d_fly t_had a_w2 d_w2".split())
        d_cur, d_cur1, d_qb, a_qb, a_k, p_k = (
            sem(n, 1) for n in "d_cur d_cur1 d_qb a_qb a_k p_k".split())
        d_xn1, t_xn1, d_h1, a_h1, d_h1lo, t_qkt, a_qkt, d_qkt = (
            sem(n, 2) for n in "d_xn1 t_xn1 d_h1 a_h1 d_h1lo t_qkt a_qkt d_qkt".split())
        t_qk, t_vg, d_rope, p_rope, a_vg, d_vlo, p_gg = (
            sem(n, TILES) for n in "t_qk t_vg d_rope p_rope a_vg d_vlo p_gg".split())
        t_s, d_p, a_p, d_plo, t_o, a_o, d_o, a_sq, p_y0, d_ss = (
            sem(n, TILES) for n in "t_s d_p a_p d_plo t_o a_o d_o a_sq p_y0 d_ss".split())
        t_kv, d_s, a_s, p_s = (sem(n, TILES - 1) for n in "t_kv d_s a_s p_s".split())
        t_yt, a_yt, d_yt, t_wo, d_wo, d_x1, d_st2, d_mv2, p_ve2, p_rs2 = (
            sem(n, 2) for n in "t_yt a_yt d_yt t_wo d_wo d_x1 d_st2 d_mv2 p_ve2 p_rs2".split())
        d_cur2, d_xn2, t_xn2, d_h2, a_h2, d_h2lo, p_vo, p_rso, d_y = (
            sem(n, 2) for n in "d_cur2 d_xn2 t_xn2 d_h2 a_h2 d_h2lo p_vo p_rso d_y".split())
        t_u1, t_u3, a_silu, d_hid, a_hid, p_hid = (
            sem(n, HB) for n in "t_u1 t_u3 a_silu d_hid a_hid p_hid".split())
        t_d = sem("t_d", HB - 1)
        t_acc, d_fin, stored = sem("t_acc", 2), sem("d_fin", 2), sem("stored", 2 * 16)
        p_x1, p_out = sem("p_x1", 2, start=1), sem("p_out", 2, start=1)

        def heads(columns):
            return columns.rearrange("p (h v) -> p h v", h=HEADS)

        def butterfly(engine, k, parts, done):
            stage, n = divmod(k, len(parts))
            cols = slice(parts[n] * D // PARTS, (parts[n] + 1) * D // PARTS)
            if k == 0:
                engine.wait_ge(in_w2.sem, 16)
            if stage:
                engine.wait_ge(done.sem, k - len(parts) + 1)
            src, dst = (t[:, :, cols].rearrange("p (g s r) d -> p g s r d", s=2, r=2 ** stage)
                        for t in ((fly0, fly1), (fly1, fly0))[stage % 2])
            engine.tensor_tensor(dst[:, :, 0], src[:, :, 0], src[:, :, 1], ALU.add)
            engine.tensor_tensor(dst[:, :, 1], src[:, :, 0], src[:, :, 1], ALU.subtract).then_inc(done.sem, 1)

        def run(engine, step):
            for kind, k in FIRST:
                step(kind, k, 0, None)
            with engine.Fori(1, B) as b:
                for kind, k in STEADY:
                    step(kind, k, b, b - 1)
            for kind, k in LAST:
                step(kind, k, None, B - 1)

        block = ctx.enter_context(nc.Block())

        @block.sync
        def _(sp):
            sp.dma_start(c_sb[:], c_t).then_inc(in_c.sem, 16)
            sp.dma_start(xres[:, 0], x[0].rearrange("(t p) d -> p t d", p=P)).then_inc(in_x0.sem, 16)
            sp.dma_start(wmod_sb[:, :, 0:2 * D], wmod[:, :, 0:2 * D]).then_inc(in_mod1.sem, 16)
            sp.dma_start(cst[:], consts).then_inc(in_cst.sem, 16)
            sp.dma_start(stage_qkvg[:], w_qkvg).then_inc(in_wqkvg.sem, 16)
            sp.dma_start(cos_sb[:], cos).then_inc(in_cos.sem, 16)
            sp.dma_start(sin_sb[:], sin).then_inc(in_sin.sem, 16)
            sp.dma_start(gnorm_in[:], gnorm).then_inc(in_gn.sem, 16)
            sp.dma_start(wmod_sb[:, :, 2 * D:6 * D], wmod[:, :, 2 * D:6 * D]).then_inc(in_mod2.sem, 16)
            sp.dma_start(sel_sb[:], select).then_inc(in_sel.sem, 16)
            sp.dma_start(fly0[:], w2).then_inc(in_w2.sem, 16)
            sp.dma_start(stage_wo[:], w_o).then_inc(in_wo.sem, 16)
            for i in range(PIECES):
                if i == 2:
                    sp.dma_start(xres[:, 1:B], x[1:B].rearrange("b (t p) d -> p (b t) d", p=P)
                                 ).then_inc(in_xr.sem, 16)
                if i >= 2:
                    sp.wait_ge(d_w13.sem, i - 1)
                sp.dma_start(stage_13[:, i % 2], w13[i]).then_inc(in_w13[i].sem, 16)

            def store(f):
                for n in range(2):
                    sp.wait_ge(p_out.sem, p_out.after(f, n + 1))
                    sp.dma_start(out[f, 2 * n * P:(2 * n + 2) * P].rearrange("(t p) d -> p t d", p=P),
                                 xres[:, f, 2 * n:2 * n + 2]).then_inc(stored.sem, 16)

            with sp.Fori(1, B) as b:
                store(b - 1)
            store(B - 1)
            sp.wait_ge(stored.sem, stored.after(B, 0))

        @block.tensor
        def _(pe):
            def three(ps, parts, start=True, stop=True):
                ops = [(a, c) for (ah, al), (ch, cl) in parts for a, c in ((ah, ch), (ah, cl), (al, ch))]
                for n, (a, c) in enumerate(ops):
                    mm = pe.matmul(ps, a, c, start=start and n == 0, stop=stop and n == len(ops) - 1,
                                   skip_group_check=True)
                return mm

            def columns(parts, at, done):
                for part in parts:
                    for h in range(KC):
                        col = part * D + h * P
                        for kc in range(KC):
                            mm = pe.matmul(pu1[:, at:at + B], wmod_sb[:, kc, col:col + P], sc_sb[:, kc, :],
                                           start=(kc == 0), stop=(kc == KC - 1))
                        at += B
                mm.then_inc(done.sem, 1)

            def step(kind, k, b, f):
                first = b == 0 if isinstance(b, int) else False
                if kind == "mod" and k == 0:
                    pe.wait_ge(in_mod1.sem, 16)
                    pe.wait_ge(a_sc.sem, 1)
                    columns((SA, CA), 0, t_cols1)
                elif kind == "mod":
                    pe.wait_ge(in_mod2.sem, 16)
                    pe.wait_ge(d_cols1.sem, 1)
                    columns((SB, CB), 2 * KC * B, t_cols2)
                elif kind == "rows":
                    pe.wait_ge(in_mod2.sem, 16)
                    for n, part in enumerate((GA, GB)):
                        for kc in range(KC):
                            mm = pe.matmul(pu3[0:B, n * D:(n + 1) * D], sc_sb[:, kc, :],
                                           wmod_sb[:, kc, part * D:(part + 1) * D],
                                           start=(kc == 0), stop=(kc == KC - 1))
                    mm.then_inc(t_rows.sem, 1)
                elif kind == "gates":
                    pe.wait_ge(in_sel.sem, 16)
                    pe.wait_ge(d_cols2.sem, 1)
                    pe.wait_ge(d_rows.sem, 4)
                    for n in range(B):
                        pe.matmul(pffn[n][:, :], sel_sb[:, n, :], gate_row,
                                  start=True, stop=True).then_inc(t_gates.sem, 1)
                elif kind == "h1":
                    if first and k == 0:
                        pe.wait_ge(in_cst.sem, 16)
                    pe.wait_ge(d_xn1.sem, d_xn1.after(b, k + 1))
                    for kc in range(KC):
                        for j in range(2):
                            mm = pe.transpose(ph1[k][:, (2 * kc + j) * P:(2 * kc + j + 1) * P],
                                              xn[:, 2 * k + j, kc * P:(kc + 1) * P], ident)
                    mm.then_inc(t_xn1.sem, 1)
                elif kind == "qk":
                    if k == 0 and first:
                        pe.wait_ge(d_wqkvg.sem, 1)
                    if k % 2 == 0:
                        pe.wait_ge(d_h1lo.sem, d_h1lo.after(b, k // 2 + 1))
                    if k:
                        pe.wait_ge(d_rope.sem, d_rope.after(b, k))
                    tok = slice(k * P, (k + 1) * P)
                    three(pa[:, 0:QK], [((h1_hi[:, kc, tok], h1_lo[:, kc, tok]),
                                         (wqkvg_hi[:, kc, 0:QK], wqkvg_lo[:, kc, 0:QK])) for kc in range(KC)]
                          ).then_inc(t_qk.sem, 1)
                elif kind == "vg":
                    if k == 1:
                        pe.wait_ge(d_h1.sem, d_h1.after(b, 2))
                    elif k >= 2:
                        pe.wait_ge(d_vlo.sem, d_vlo.after(b, k - 1))
                    tok = slice(k * P, (k + 1) * P)
                    three(pvg[k % 2][:, :], [((h1_hi[:, kc, tok], h1_lo[:, kc, tok]),
                                              (wqkvg_hi[:, kc, QK:QK + VG], wqkvg_lo[:, kc, QK:QK + VG]))
                                             for kc in range(KC)]).then_inc(t_vg.sem, 1)
                elif kind == "qt":
                    pe.wait_ge(p_rope.sem, p_rope.after(b, TILES))
                    for t in range(TILES):
                        mm = pe.transpose(pa[:, t * P:(t + 1) * P], qk[:, t, 0:P], ident)
                    mm.then_inc(t_qkt.sem, 1)
                elif kind == "kt":
                    pe.wait_ge(d_vlo.sem, d_vlo.after(b, TILES))
                    for t in range(TILES):
                        mm = pe.transpose(pb[:, t * P:(t + 1) * P], qk[:, t, P:2 * P], ident)
                    mm.then_inc(t_qkt.sem, 1)
                elif kind == "score":
                    if k == 0:
                        pe.wait_ge(d_qb.sem, d_qb.after(b, 1))
                        pe.wait_ge(a_qb.sem, a_qb.after(b, 1))
                    else:
                        pe.wait_ge(d_p.sem, d_p.after(b, k))
                    three(pc[:, :], [((kt_hi[:, k], kt_lo[:, k]), (qb_hi[:, k], qb_lo[:, k]))]
                          ).then_inc(t_s.sem, 1)
                elif kind == "state":
                    if k == 0:
                        pe.wait_ge(p_k.sem, p_k.after(b, 1))
                    else:
                        pe.wait_ge(d_s.sem, d_s.after(b, k))
                    three(pstate[:, 0:HEADS * DV], [((k_hi[:, k], k_lo[:, k]), (v_hi[:, k], v_lo[:, k]))],
                          start=(k == 0)).then_inc(t_kv.sem, 1)
                elif kind == "o":
                    if k >= 2:
                        pe.wait_ge(d_o.sem, d_o.after(b, k - 1))
                    out_k = po[k % 2][:, :].rearrange("p (h s v) -> p h s v", h=HEADS, s=2)
                    if k:
                        pe.wait_ge(p_s.sem, p_s.after(b, k))
                        three(out_k[:, :, 0], [((qt_hi[:, k], qt_lo[:, k]),
                                                (s_hi[:, (k - 1) % 2], s_lo[:, (k - 1) % 2]))], stop=False)
                    pe.wait_ge(d_plo.sem, d_plo.after(b, k + 1))
                    for h in range(HEADS):
                        pe.matmul(out_k[:, h], p_hi[:, k % 2, h], v2[:, k, h], start=(k == 0 and h == 0), stop=False,
                                  skip_group_check=True)
                        mm = pe.matmul(out_k[:, h, 0], p_lo[:, k % 2, h], v2[:, k, h, 0], start=False,
                                       stop=(h == HEADS - 1), skip_group_check=True)
                    mm.then_inc(t_o.sem, 1)
                elif kind == "yt":
                    pe.wait_ge(d_y.sem, d_y.after(b, k + 1))
                    for kc in range(KC):
                        for j in range(2):
                            mm = pe.transpose(py[k][:, (2 * kc + j) * P:(2 * kc + j + 1) * P],
                                              xn[:, 2 * k + j, kc * P:(kc + 1) * P], ident)
                    mm.then_inc(t_yt.sem, 1)
                elif kind == "proj":
                    pe.wait_ge(d_yt.sem, d_yt.after(b, k + 1))
                    if k == 0:
                        pe.wait_ge(d_o.sem, d_o.after(b, 3))
                        if first:
                            pe.wait_ge(d_wo_lo.sem, 1)
                    for j in range(2):
                        tok = slice((2 * k + j) * P, (2 * k + j + 1) * P)
                        mm = three(pw[k][:, j * D:(j + 1) * D],
                                   [((h1_hi[:, kc, tok], h1_lo[:, kc, tok]), (wo_hi[:, kc], wo_lo[:, kc]))
                                    for kc in range(KC)])
                    mm.then_inc(t_wo.sem, 1)
                elif kind == "h2":
                    pe.wait_ge(d_xn2.sem, d_xn2.after(b, k + 1))
                    for kc in range(KC):
                        for j in range(2):
                            mm = pe.transpose(ph2[k][:, (2 * kc + j) * P:(2 * kc + j + 1) * P],
                                              xn[:, 2 * k + j, kc * P:(kc + 1) * P], ident)
                    mm.then_inc(t_xn2.sem, 1)
                elif kind == "had":
                    pe.wait_ge(a_gates.sem, B)
                    pe.wait_ge(d_fly.sem, 1)
                    for n, ps in enumerate(pffn):
                        pe.matmul(ps[:, :], had_r[:], w2_hi[:, 2 * n:2 * n + 2, :], start=True, stop=False)
                        pe.matmul(ps[:, :], had_r[:], w2_lo[:, 2 * n:2 * n + 2, :], start=False, stop=True
                                  ).then_inc(t_had.sem, 1)
                elif kind == "up":
                    if k == 0:
                        pe.wait_ge(d_h2lo.sem, d_h2lo.after(f, KC))
                        pe.wait_ge(d_w2.sem, len(pffn))
                        pe.wait_ge(d_w13.sem, PIECES)
                    piece, col = divmod(k * P, PW)
                    for w, ps, read, done in ((0, pu1, a_silu, t_u1), (1, pu3, d_hid, t_u3)):
                        if k:
                            pe.wait_ge(read.sem, read.after(f, k))
                        three(ps[:, :], [((w13_hi[:, piece, w, kc, col:col + P],
                                           w13_lo[:, piece, w, kc, col:col + P]),
                                          (h2_hi[:, kc], h2_lo[:, kc])) for kc in range(KC)]
                              ).then_inc(done.sem, 1)
                elif kind == "down":
                    if k == 0 and isinstance(f, int):
                        pe.wait_ge(d_fin.sem, d_fin.after(f, 0))
                    pe.wait_ge(p_hid.sem, p_hid.after(f, k + 1))
                    for t in range(TILES):
                        tok = slice(t * P, (t + 1) * P)
                        mm = three(pacc[t // 2][:, t % 2 * D:(t % 2 + 1) * D],
                                   [((hid_hi[:, k % 2, tok], hid_lo[:, k % 2, tok]), (w2_hi[:, k], w2_lo[:, k]))],
                                   start=(k == 0 and t % 2 == 0), stop=(k == HB - 1))
                        if k == HB - 1 and t % 2:
                            mm.then_inc(t_acc.sem, 1)
                    if k < HB - 1:
                        mm.then_inc(t_d.sem, 1)

            run(pe, step)

        @block.vector
        def _(dve):
            def step(kind, k, b, f):
                first = b == 0 if isinstance(b, int) else False
                if kind == "stats":
                    dve.wait_ge((in_xr if k else in_x0).sem, 16)
                    if k:
                        dve.wait_ge(d_mv1.sem, k)
                    for t in range(TILES):
                        ins = dve.bn_stats(stats1[:, t, :], xres[:, k, t])
                    ins.then_inc(d_st1.sem, 1)
                    dve.wait_ge(d_st1.sem, k + 1)
                    for t in range(TILES):
                        ins = dve.bn_aggr(mv1[:, k, t], stats1[:, t, :])
                    ins.then_inc(d_mv1.sem, 1)
                elif kind == "mod" and k == 0:
                    dve.wait_ge(t_cols1.sem, 1)
                    for n, add in ((0, 0.0), (1, 1.0)):
                        ins = dve.tensor_scalar(mod_cols[:, :, n, :], pu1[:, n * KC * B:(n + 1) * KC * B].rearrange(
                            "p (h b) -> p b h", b=B), add, None, ALU.add)
                    ins.then_inc(d_cols1.sem, 1)
                elif kind == "mod":
                    dve.wait_ge(t_cols2.sem, 1)
                    for n, add in ((2, 0.0), (3, 1.0)):
                        ins = dve.tensor_scalar(mod_cols[:, :, n, :], pu1[:, n * KC * B:(n + 1) * KC * B].rearrange(
                            "p (h b) -> p b h", b=B), add, None, ALU.add)
                    ins.then_inc(d_cols2.sem, 1)
                elif kind == "rows":
                    dve.wait_ge(t_rows.sem, 1)
                    dve.tensor_scalar(gate_row, pu3[0:B, :], 0.0, 2.0, ALU.is_ge, ALU.mult
                                      ).then_inc(d_rows.sem, 1)
                    dve.wait_ge(d_rows.sem, 1)
                    dve.scalar_tensor_tensor(out=gate_size, in0=gate_row, scalar=-1.0, in1=pu3[0:B, :],
                                             op0=ALU.add, op1=ALU.mult).then_inc(d_rows.sem, 1)
                    dve.wait_ge(d_rows.sem, 2)
                    dve.tensor_scalar(gate_size, gate_size, MIN_GATE, None, ALU.max).then_inc(d_rows.sem, 1)
                    dve.wait_ge(d_rows.sem, 3)
                    dve.scalar_tensor_tensor(out=gate_row, in0=gate_row, scalar=-1.0, in1=gate_size,
                                             op0=ALU.add, op1=ALU.mult).then_inc(d_rows.sem, 1)
                elif kind == "w_lo":
                    dve.wait_ge(a_wqkvg.sem, 1)
                    dve.tensor_tensor(wqkvg_lo[:], stage_qkvg[:], wqkvg_hi[:].bitcast(F32), ALU.subtract
                                      ).then_inc(d_wqkvg.sem, 1)
                elif kind == "w_o":
                    dve.wait_ge(a_wo.sem, 1)
                    dve.tensor_tensor(wo_lo[:], stage_wo[:], wo_hi[:].bitcast(F32), ALU.subtract
                                      ).then_inc(d_wo_lo.sem, 1)
                elif kind == "w_w13":
                    dve.wait_ge(a_w13.sem, k + 1)
                    dve.tensor_tensor(w13_lo[:, k], stage_13[:, k % 2], w13_hi[:, k].bitcast(F32), ALU.subtract
                                      ).then_inc(d_w13.sem, 1)
                elif kind == "fly_a":
                    butterfly(dve, k, FLY_A, d_flya)
                elif kind == "fold":
                    dve.wait_ge(a_fly.sem, 1)
                    dve.tensor_tensor(w2_lo[:], fly1[:], w2_hi[:].bitcast(F32), ALU.subtract
                                      ).then_inc(d_fly.sem, 1)
                elif kind == "had":
                    for n, ps in enumerate(pffn):
                        dve.wait_ge(a_w2.sem, n + 1)
                        dve.scalar_tensor_tensor(out=w2_lo[:, 2 * n:2 * n + 2, :], in0=ps[:, :].rearrange(
                            "p (n d) -> p n d", n=2), scalar=HID ** -0.5,
                            in1=w2_hi[:, 2 * n:2 * n + 2, :].bitcast(F32), op0=ALU.mult, op1=ALU.subtract
                            ).then_inc(d_w2.sem, 1)
                elif kind == "norm":
                    if k == 0:
                        dve.wait_ge(p_rs1.sem, 1 if first else B)
                        dve.wait_ge(d_mv1.sem, 1 if first else B)
                        dve.tensor_copy(rs_cur[:], rs1[:, b])
                        dve.tensor_copy(mv_cur[:], mv1[:, b]).then_inc(d_cur.sem, 1)
                        dve.wait_ge(d_cur.sem, d_cur.after(b, 1))
                    for t in (2 * k, 2 * k + 1):
                        ins = dve.tensor_scalar(xn[:, t], xres[:, b, t], mv_cur[:, t, 0:1], rs_cur[:, t:t + 1],
                                                ALU.subtract, ALU.mult)
                    ins.then_inc(d_xn1.sem, 1)
                elif kind == "h1":
                    if k == 0:
                        if first:
                            dve.wait_ge(d_cols1.sem, 1)
                        dve.tensor_copy(mod_cur[:, 0:2], mod_cols[:, b, 0:2]).then_inc(d_cur1.sem, 1)
                        dve.wait_ge(d_cur1.sem, d_cur1.after(b, 1))
                    dve.wait_ge(t_xn1.sem, t_xn1.after(b, k + 1))
                    for kc in range(KC):
                        ins = dve.tensor_scalar(h32[:, kc, 2 * k * P:(2 * k + 2) * P],
                                                ph1[k][:, 2 * kc * P:(2 * kc + 2) * P], mod_cur[:, 1, kc:kc + 1],
                                                mod_cur[:, 0, kc:kc + 1], ALU.mult, ALU.add)
                    ins.then_inc(d_h1.sem, 1)
                elif kind == "h1lo":
                    tok = slice(2 * k * P, (2 * k + 2) * P)
                    dve.wait_ge(a_h1.sem, a_h1.after(b, k + 1))
                    dve.tensor_tensor(h1_lo[:, :, tok], h32[:, :, tok], h1_hi[:, :, tok].bitcast(F32), ALU.subtract
                                      ).then_inc(d_h1lo.sem, 1)
                elif kind == "qk":
                    if first and k == 0:
                        dve.wait_ge(in_cos.sem, 16)
                        dve.wait_ge(in_sin.sem, 16)
                    dve.wait_ge(t_qk.sem, t_qk.after(b, k + 1))
                    if k >= 2 or not first:
                        dve.wait_ge(p_rope.sem, p_rope.after(b, k - 1))
                    dve.tensor_tensor(rope_a[:, k % 2], pa[:, 0:QK], cos_sb[:, k], ALU.mult)
                    halves = [t.rearrange("p (g s e) -> p g s e", s=2, e=DK // 2)
                              for t in (rope_b[:, k % 2], pa[:, 0:QK], sin_sb[:, k])]
                    for s in range(2):
                        ins = dve.tensor_tensor(halves[0][:, :, 1 - s], halves[1][:, :, s], halves[2][:, :, s],
                                                ALU.mult)
                    ins.then_inc(d_rope.sem, 1)
                elif kind == "vg":
                    dve.wait_ge(a_vg.sem, a_vg.after(b, k + 1))
                    dve.tensor_tensor(v_lo[:, k], heads(pvg[k % 2][:, 0:D]), v_hi[:, k].bitcast(F32), ALU.subtract
                                      ).then_inc(d_vlo.sem, 1)
                elif kind in ("qt", "kt"):
                    n, ps, hi, lo = (0, pa, qt_hi, qt_lo) if kind == "qt" else (1, pb, kt_hi, kt_lo)
                    dve.wait_ge(a_qkt.sem, a_qkt.after(b, n + 1))
                    dve.tensor_tensor(lo[:], ps[:, :].rearrange("p (t i) -> p t i", t=TILES),
                                      hi[:].bitcast(F32), ALU.subtract).then_inc(d_qkt.sem, 1)
                elif kind == "qblk":
                    if first:
                        dve.wait_ge(p_zero.sem, 2)
                    for h in range(HEADS):
                        rows = slice(h * DK, (h + 1) * DK)
                        ins = dve.tensor_copy(qb_hi[rows, :, h, :], qt_hi[rows].bitcast(F32))
                    ins.then_inc(d_qb.sem, 1)
                elif kind == "score":
                    if k >= 2:
                        dve.wait_ge(d_plo.sem, d_plo.after(b, k - 1))
                    dve.wait_ge(t_s.sem, t_s.after(b, k + 1))
                    dve.tensor_tensor(p32[:, k % 2], pc[:, :].rearrange("p (h i) -> p h i", h=HEADS),
                                      causal.unsqueeze(1).to_broadcast([P, HEADS, P]), ALU.mult
                                      ).then_inc(d_p.sem, 1)
                elif kind == "plo":
                    dve.wait_ge(a_p.sem, a_p.after(b, k + 1))
                    dve.tensor_tensor(p_lo[:, k % 2], p32[:, k % 2], p_hi[:, k % 2].bitcast(F32), ALU.subtract
                                      ).then_inc(d_plo.sem, 1)
                elif kind == "state":
                    dve.wait_ge(t_kv.sem, t_kv.after(b, k + 1))
                    if k:
                        dve.wait_ge(p_s.sem, p_s.after(b, k))
                    dve.tensor_tensor(s32[:], pstate[:, 0:HEADS * DV], blocks, ALU.mult).then_inc(d_s.sem, 1)
                elif kind == "o":
                    dve.wait_ge(a_o.sem, a_o.after(b, k + 1))
                    parts = po[k % 2][:, :].rearrange("p (h s v) -> p h s v", h=HEADS, s=2)
                    dve.tensor_tensor(heads(xn[:, k]), parts[:, :, 0], heads(xn[:, k]), ALU.add).then_inc(d_o.sem, 1)
                elif kind == "ss":
                    dve.wait_ge(a_sq.sem, a_sq.after(b, k + 1))
                    dve.reduce_sum(ss[:, k], heads(sq[:, k % 2]), AX.X).then_inc(d_ss.sem, 1)
                elif kind == "rms":
                    dve.wait_ge(p_rso.sem, p_rso.after(b, k + 1))
                    pair = slice(2 * k, 2 * k + 2)
                    y = xn[:, pair].rearrange("p t (h v) -> p (t h) v", h=HEADS)
                    dve.wait_ge(p_y0.sem, p_y0.after(b, 2 * k + 2))
                    dve.tensor_tensor(y, y, rso[:, pair].rearrange("p t h -> p (t h)").unsqueeze(2).to_broadcast(
                        [P, 2 * HEADS, DV]), ALU.mult).then_inc(d_y.sem, 1)
                elif kind == "yt":
                    dve.wait_ge(a_yt.sem, a_yt.after(b, k + 1))
                    tok = slice(2 * k * P, (2 * k + 2) * P)
                    dve.tensor_tensor(h1_lo[:, :, tok], py[k][:, :].rearrange("p (k n) -> p k n", k=KC),
                                      h1_hi[:, :, tok].bitcast(F32), ALU.subtract).then_inc(d_yt.sem, 1)
                elif kind == "proj":
                    dve.wait_ge(t_wo.sem, t_wo.after(b, k + 1))
                    if first and k == 0:
                        dve.wait_ge(a_gates.sem, B)
                    pair = slice(2 * k, 2 * k + 2)
                    dve.tensor_tensor(branch[k][:], pw[k][:, :].rearrange("p (t d) -> p t d", t=2),
                                      gates[:, b, 0].unsqueeze(1).to_broadcast([P, 2, D]), ALU.mult
                                      ).then_inc(d_wo.sem, 1)
                    dve.wait_ge(d_wo.sem, d_wo.after(b, k + 1))
                    dve.tensor_tensor(x1[:, pair], xres[:, b, pair], branch[k][:], ALU.add).then_inc(d_x1.sem, 1)
                    dve.wait_ge(d_x1.sem, d_x1.after(b, k + 1))
                    for t in (2 * k, 2 * k + 1):
                        ins = dve.bn_stats(stats[:, t, :], x1[:, t])
                    ins.then_inc(d_st2.sem, 1)
                    dve.wait_ge(d_st2.sem, d_st2.after(b, k + 1))
                    if first and k == 0:
                        dve.wait_ge(d_cols2.sem, 1)
                    dve.tensor_scalar(mod_cur[:, 2 + k], mod_cols[:, b, 2 + k], 1.0, None, ALU.mult
                                      ).then_inc(d_cur2.sem, 1)
                    for t in (2 * k, 2 * k + 1):
                        ins = dve.bn_aggr(mv2[:, t], stats[:, t, :])
                    ins.then_inc(d_mv2.sem, 1)
                elif kind == "norm2":
                    dve.wait_ge(p_rs2.sem, p_rs2.after(b, k + 1))
                    for t in (2 * k, 2 * k + 1):
                        ins = dve.tensor_scalar(xn[:, t], x1[:, t], mv2[:, t, 0:1], rs2[:, t:t + 1],
                                                ALU.subtract, ALU.mult)
                    ins.then_inc(d_xn2.sem, 1)
                elif kind == "h2":
                    if k == 0:
                        dve.wait_ge(d_cur2.sem, d_cur2.after(b, 2))
                    dve.wait_ge(t_xn2.sem, t_xn2.after(b, k + 1))
                    for kc in range(KC):
                        ins = dve.tensor_scalar(h32[:, kc, 2 * k * P:(2 * k + 2) * P],
                                                ph2[k][:, 2 * kc * P:(2 * kc + 2) * P], mod_cur[:, 3, kc:kc + 1],
                                                mod_cur[:, 2, kc:kc + 1], ALU.mult, ALU.add)
                    ins.then_inc(d_h2.sem, 1)
                elif kind == "h2lo":
                    tok = slice(2 * k * P, (2 * k + 2) * P)
                    dve.wait_ge(a_h2.sem, a_h2.after(b, k + 1))
                    dve.tensor_tensor(h2_lo[:, :, tok], h32[:, :, tok], h2_hi[:, :, tok].bitcast(F32), ALU.subtract
                                      ).then_inc(d_h2lo.sem, 1)
                elif kind == "up":
                    dve.wait_ge(t_u3.sem, t_u3.after(f, k + 1))
                    dve.wait_ge(a_silu.sem, a_silu.after(f, k + 1))
                    if k >= 2:
                        dve.wait_ge(p_hid.sem, p_hid.after(f, k - 1))
                    else:
                        dve.wait_ge(p_out.sem, p_out.after(f, 0))
                    dve.tensor_tensor(hid32[:, k % 2], silu1[:, k % 2], pu3[:, :], ALU.mult
                                      ).then_inc(d_hid.sem, 1)
                elif kind == "out":
                    dve.wait_ge(t_acc.sem, t_acc.after(f, k + 1))
                    dve.tensor_tensor(hid32[:, k].rearrange("p (t d) -> p t d", t=2),
                                      pacc[k][:, :].rearrange("p (t d) -> p t d", t=2),
                                      gates[:, f, 1].unsqueeze(1).to_broadcast([P, 2, D]), ALU.mult
                                      ).then_inc(d_fin.sem, 1)

            run(dve, step)

        @block.scalar
        def _(act):
            act.wait_ge(in_c.sem, 16)
            act.activation(sc_sb[:], c_sb[:], ACT.Silu).then_inc(a_sc.sem, 1)
            act.wait_ge(in_gn.sem, 16)
            act.activation(gnorm_sb[:], gnorm_in[:], ACT.Copy, scale=DV ** 0.5).then_inc(a_gn.sem, 1)

            def step(kind, k, b, f):
                first = b == 0 if isinstance(b, int) else False
                if kind == "w_hi":
                    act.wait_ge(in_wqkvg.sem, 16)
                    act.activation(wqkvg_hi[:], stage_qkvg[:], ACT.Copy).then_inc(a_wqkvg.sem, 1)
                    act.wait_ge(in_cst.sem, 16)
                    act.activation(had_r[:], hadamard, ACT.Copy).then_inc(a_had.sem, 1)
                elif kind == "w_o":
                    act.wait_ge(in_wo.sem, 16)
                    act.activation(wo_hi[:], stage_wo[:], ACT.Copy).then_inc(a_wo.sem, 1)
                elif kind == "w_w13":
                    act.wait_ge(in_w13[k].sem, 16)
                    act.activation(w13_hi[:, k], stage_13[:, k % 2], ACT.Copy).then_inc(a_w13.sem, 1)
                elif kind == "gates":
                    for n in range(B):
                        act.wait_ge(t_gates.sem, n + 1)
                        act.activation(gates[:, n].rearrange("p g d -> p (g d)"), pffn[n][:, :], ACT.Copy
                                       ).then_inc(a_gates.sem, 1)
                elif kind == "fold":
                    act.wait_ge(d_flya.sem, STAGES * len(FLY_A))
                    act.wait_ge(p_fly.sem, STAGES * len(FLY_B))
                    act.activation(w2_hi[:], fly1[:], ACT.Copy).then_inc(a_fly.sem, 1)
                elif kind == "had":
                    act.wait_ge(t_had.sem, len(pffn))
                    for n, ps in enumerate(pffn):
                        act.activation(w2_hi[:, 2 * n:2 * n + 2, :], ps[:, :].rearrange("p (n d) -> p n d", n=2),
                                       ACT.Copy, scale=HID ** -0.5).then_inc(a_w2.sem, 1)
                elif kind == "h1":
                    tok = slice(2 * k * P, (2 * k + 2) * P)
                    act.wait_ge(d_h1.sem, d_h1.after(b, k + 1))
                    act.activation(h1_hi[:, :, tok], h32[:, :, tok], ACT.Copy).then_inc(a_h1.sem, 1)
                elif kind == "vg":
                    act.wait_ge(t_vg.sem, t_vg.after(b, k + 1))
                    act.activation(v_hi[:, k], heads(pvg[k % 2][:, 0:D]), ACT.Copy)
                    if k >= 2:
                        act.wait_ge(p_gg.sem, p_gg.after(b, k - 1))
                    act.activation(g32[:, k % 2], pvg[k % 2][:, D:2 * D], ACT.Silu).then_inc(a_vg.sem, 1)
                elif kind in ("qt", "kt"):
                    n, ps, hi = (0, pa, qt_hi) if kind == "qt" else (1, pb, kt_hi)
                    act.wait_ge(t_qkt.sem, t_qkt.after(b, n + 1))
                    act.activation(hi[:], ps[:, :].rearrange("p (t i) -> p t i", t=TILES), ACT.Copy
                                   ).then_inc(a_qkt.sem, 1)
                elif kind == "ksplit":
                    act.wait_ge(p_rope.sem, p_rope.after(b, TILES))
                    act.activation(k_hi[:], qk[:, :, P:2 * P], ACT.Copy).then_inc(a_k.sem, 1)
                elif kind == "qblk":
                    if first:
                        act.wait_ge(p_zero.sem, 2)
                    act.wait_ge(d_qkt.sem, d_qkt.after(b, 1))
                    for h in range(HEADS):
                        rows = slice(h * DK, (h + 1) * DK)
                        ins = act.activation(qb_lo[rows, :, h, :], qt_lo[rows].bitcast(F32), ACT.Copy)
                    ins.then_inc(a_qb.sem, 1)
                elif kind == "score":
                    if k >= 2:
                        act.wait_ge(t_o.sem, t_o.after(b, k - 1))
                    act.wait_ge(d_p.sem, d_p.after(b, k + 1))
                    act.activation(p_hi[:, k % 2], p32[:, k % 2], ACT.Copy).then_inc(a_p.sem, 1)
                elif kind == "state":
                    if k >= 2:
                        act.wait_ge(t_o.sem, t_o.after(b, k))
                    act.wait_ge(d_s.sem, d_s.after(b, k + 1))
                    act.activation(s_hi[:, k % 2], s32[:], ACT.Copy).then_inc(a_s.sem, 1)
                elif kind == "o":
                    act.wait_ge(t_o.sem, t_o.after(b, k + 1))
                    act.activation(heads(xn[:, k]), po[k % 2][:, :].rearrange("p (h s v) -> p h s v", h=HEADS, s=2
                                                                              )[:, :, 1], ACT.Copy
                                   ).then_inc(a_o.sem, 1)
                elif kind == "ss":
                    act.wait_ge(d_o.sem, d_o.after(b, k + 1))
                    if k >= 2:
                        act.wait_ge(d_ss.sem, d_ss.after(b, k - 1))
                    act.activation(sq[:, k % 2], xn[:, k], ACT.Square).then_inc(a_sq.sem, 1)
                elif kind == "yt":
                    act.wait_ge(t_yt.sem, t_yt.after(b, k + 1))
                    act.activation(h1_hi[:, :, 2 * k * P:(2 * k + 2) * P],
                                   py[k][:, :].rearrange("p (k n) -> p k n", k=KC), ACT.Copy).then_inc(a_yt.sem, 1)
                elif kind == "h2":
                    tok = slice(2 * k * P, (2 * k + 2) * P)
                    act.wait_ge(d_h2.sem, d_h2.after(b, k + 1))
                    act.activation(h2_hi[:, :, tok], h32[:, :, tok], ACT.Copy).then_inc(a_h2.sem, 1)
                elif kind == "up":
                    act.wait_ge(t_u1.sem, t_u1.after(f, k + 1))
                    if k >= 2:
                        act.wait_ge(d_hid.sem, d_hid.after(f, k - 1))
                    act.activation(silu1[:, k % 2], pu1[:, :], ACT.Silu).then_inc(a_silu.sem, 1)
                elif kind == "hid":
                    act.wait_ge(d_hid.sem, d_hid.after(f, k + 1))
                    if k >= 2:
                        act.wait_ge(t_d.sem, t_d.after(f, k - 1))
                    act.activation(hid_hi[:, k % 2], hid32[:, k % 2], ACT.Copy).then_inc(a_hid.sem, 1)

            run(act, step)

        @block.gpsimd
        def _(pool):
            pool.memset(eps_ln[:], EPS).then_inc(p_mhalf.sem, 1)
            pool.memset(unused[:, 0:1], 0.0).then_inc(p_x1.sem, 1)
            pool.memset(unused[:, 1:2], 0.0).then_inc(p_out.sem, 1)
            pool.memset(eps_rms[:], DV * EPS).then_inc(p_mhalf.sem, 1)
            pool.memset(mhalf[:], -0.5).then_inc(p_mhalf.sem, 1)

            def step(kind, k, b, f):
                first = b == 0 if isinstance(b, int) else False
                if kind == "stats":
                    pool.wait_ge(p_mhalf.sem, 3)
                    pool.wait_ge(d_mv1.sem, k + 1)
                    pool.tensor_tensor(ve1[:, k], mv1[:, k, :, 1], eps_ln[:], ALU.add).then_inc(p_ve1.sem, 1)
                    pool.wait_ge(p_ve1.sem, k + 1)
                    pool.tensor_tensor(rs1[:, k], ve1[:, k], mhalf[:, 0:TILES], ALU.pow).then_inc(p_rs1.sem, 1)
                elif kind == "zero":
                    pool.wait_ge(t_cols2.sem, 1)
                    pool.wait_ge(t_rows.sem, 1)
                    pool.wait_ge(d_wqkvg.sem, 1)
                    pool.memset(qb_hi[:].bitcast(F32), 0.0).then_inc(p_zero.sem, 1)
                    pool.memset(qb_lo[:].bitcast(F32), 0.0).then_inc(p_zero.sem, 1)
                elif kind == "fly_b":
                    butterfly(pool, k, FLY_B, p_fly)
                elif kind == "qk":
                    pool.wait_ge(d_rope.sem, d_rope.after(b, k + 1))
                    pool.tensor_tensor(qk[:, k], rope_a[:, k % 2], rope_b[:, k % 2], ALU.add
                                       ).then_inc(p_rope.sem, 1)
                elif kind == "vg":
                    if first and k == 0:
                        pool.wait_ge(a_gn.sem, 1)
                    pool.wait_ge(a_vg.sem, a_vg.after(b, k + 1))
                    pool.tensor_tensor(gg[:, k].rearrange("p (h v) -> p h v", h=HEADS),
                                       g32[:, k % 2].rearrange("p (h v) -> p h v", h=HEADS),
                                       gnorm_sb[:].unsqueeze(1).to_broadcast([P, HEADS, DV]), ALU.mult
                                       ).then_inc(p_gg.sem, 1)
                elif kind == "ksplit":
                    pool.wait_ge(a_k.sem, a_k.after(b, 1))
                    pool.tensor_tensor(k_lo[:], qk[:, :, P:2 * P], k_hi[:].bitcast(F32), ALU.subtract
                                       ).then_inc(p_k.sem, 1)
                elif kind == "state":
                    pool.wait_ge(a_s.sem, a_s.after(b, k + 1))
                    pool.tensor_tensor(s_lo[:, k % 2], s32[:], s_hi[:, k % 2].bitcast(F32), ALU.subtract
                                       ).then_inc(p_s.sem, 1)
                elif kind == "ss":
                    pool.wait_ge(a_sq.sem, a_sq.after(b, k + 1))
                    pool.tensor_tensor(xn[:, k], xn[:, k], gg[:, k], ALU.mult).then_inc(p_y0.sem, 1)
                elif kind == "rms":
                    s2, v2, r2 = (t[:, 2 * k:2 * k + 2].rearrange("p t h -> p (t h)") for t in (ss, vo, rso))
                    pool.wait_ge(d_ss.sem, d_ss.after(b, 2 * k + 2))
                    pool.tensor_tensor(v2, s2, eps_rms[:], ALU.add).then_inc(p_vo.sem, 1)
                    pool.wait_ge(p_vo.sem, p_vo.after(b, k + 1))
                    pool.tensor_tensor(r2, v2, mhalf[:], ALU.pow).then_inc(p_rso.sem, 1)
                elif kind == "proj":
                    pair = slice(2 * k, 2 * k + 2)
                    pool.wait_ge(d_mv2.sem, d_mv2.after(b, k + 1))
                    pool.tensor_tensor(ve2[:, pair], mv2[:, pair, 1], eps_ln[:, 0:2], ALU.add).then_inc(p_ve2.sem, 1)
                    pool.wait_ge(p_ve2.sem, p_ve2.after(b, k + 1))
                    pool.tensor_tensor(rs2[:, pair], ve2[:, pair], mhalf[:, 0:2], ALU.pow).then_inc(p_rs2.sem, 1)
                    pool.tensor_tensor(xres[:, b, pair], xres[:, b, pair], branch[k][:], ALU.add
                                       ).then_inc(p_x1.sem, 1)
                elif kind == "hid":
                    pool.wait_ge(a_hid.sem, a_hid.after(f, k + 1))
                    pool.tensor_tensor(hid_lo[:, k % 2], hid32[:, k % 2], hid_hi[:, k % 2].bitcast(F32),
                                       ALU.subtract).then_inc(p_hid.sem, 1)
                elif kind == "out":
                    pair = slice(2 * k, 2 * k + 2)
                    pool.wait_ge(p_x1.sem, p_x1.after(f, 2))
                    pool.wait_ge(d_fin.sem, d_fin.after(f, k + 1))
                    pool.tensor_tensor(xres[:, f, pair], xres[:, f, pair], hid32[:, k].rearrange(
                        "p (t d) -> p t d", t=2), ALU.add).then_inc(p_out.sem, 1)

            run(pool, step)


def constants():
    i = np.arange(P)
    head = np.arange(QK) % P // DK
    consts = np.zeros((P, C_END), np.float32)
    consts[:, C_IDENT:C_IDENT + P] = np.eye(P)
    consts[:, C_CAUSAL:C_CAUSAL + P] = i[None, :] >= i[:, None]
    bits = np.array([[bin(r & c).count("1") for c in range(P)] for r in range(P)])
    consts[:, C_HADAMARD:C_HADAMARD + P] = 1 - 2 * (bits % 2)
    consts[:, C_BLOCKS:C_END] = i[:, None] // DK == np.arange(HEADS * DV)[None, :] // DV
    select = np.zeros((B, B, P), np.float32)
    for b in range(B):
        select[b, b] = 1
    inv_freq = (np.float32(1) / np.float32(10000) ** (np.arange(0, DK, 2, dtype=np.float32) / np.float32(DK)))
    angle = (np.arange(N, dtype=np.float32)[:, None] * inv_freq.astype(np.float32)).astype(np.float64)
    angle = angle[:, np.arange(QK) % (DK // 2)]
    gamma = 1.0 - 2.0 ** (-5.0 - head)
    is_q = np.arange(QK) < P
    power = np.arange(N)[:, None] * np.where(is_q, 1.0, -1.0)
    factor = gamma ** power * np.where(is_q, DK ** -0.5, 1.0)
    sign = np.where(np.arange(QK) % DK < DK // 2, 1.0, -1.0)
    tile = lambda a: np.ascontiguousarray(a.astype(np.float32).reshape(TILES, P, QK).transpose(1, 0, 2))
    return consts, select, tile(np.cos(angle) * factor), tile(np.sin(angle) * factor * sign)


def rows_to_partitions(w):
    return np.ascontiguousarray(w.reshape(-1, P, w.shape[1]).transpose(1, 0, 2))


def kernel(L0_attn_x, L0_attn_Wq, L0_attn_Wk, L0_attn_Wv, L0_attn_Wg, L0_attn_Wo, L0_attn_gnorm_w,
           L0_ffn_W1, L0_ffn_W2, L0_ffn_W3, L0_c, L0_wmod):
    import concourse.bacc as bacc
    from concourse.bass_utils import run_bass_kernel_spmd

    arr = np.asarray
    w_qkvg = rows_to_partitions(np.concatenate([arr(w) for w in (L0_attn_Wq, L0_attn_Wk, L0_attn_Wv, L0_attn_Wg)]).T)
    w13 = np.stack([rows_to_partitions(arr(w).T) for w in (L0_ffn_W1, L0_ffn_W3)])
    w13 = np.ascontiguousarray(w13.reshape(2, P, KC, PIECES, PW).transpose(3, 1, 0, 2, 4))
    consts, select, cos, sin = constants()
    arrays = {
        "x": arr(L0_attn_x),
        "c_t": rows_to_partitions(arr(L0_c).T),
        "w_qkvg": w_qkvg,
        "w_o": rows_to_partitions(arr(L0_attn_Wo).T),
        "gnorm": np.ascontiguousarray(np.broadcast_to(arr(L0_attn_gnorm_w), (P, DV))),
        "w13": w13,
        "w2": rows_to_partitions(arr(L0_ffn_W2).T),
        "wmod": rows_to_partitions(arr(L0_wmod)),
        "consts": consts, "select": select, "cos": cos, "sin": sin,
    }
    nc = bacc.Bacc("TRN2", target_bir_lowering=False, num_devices=1)
    args = [nc.dram_tensor(name, a.shape, mybir.dt.from_np(a.dtype), kind="ExternalInput").ap()
            for name, a in arrays.items()]
    args.append(nc.dram_tensor("out", (B, N, D), F32, kind="ExternalOutput").ap())
    adaln_block_kernel(nc, *args)
    return run_bass_kernel_spmd(nc, [arrays], core_ids=[0]).results[0]["out"]
```

```python
from contextlib import ExitStack

import numpy as np

import concourse.bass as bass
from concourse import mybir

P = 128
B, N, D = 4, 512, 256
HEADS, DK, DV = 4, 32, 64
HID = 1024
TILES = N // P
KC = D // P
QK = 2 * HEADS * DK
VG = 2 * HEADS * DV
HB = HID // P
PIECES = 4
PW = HID // PIECES
STAGES, PARTS = 3, 4
FLY_A, FLY_B = (0, 1), (2, 3)
W13_A, W13_B = (0, 1), (2, 3)
EPS = 1e-5
MIN_GATE = 0.25
SA, CA, GA, SB, CB, GB = range(6)

F32 = mybir.dt.float32
F32R = mybir.dt.float32r
ALU = mybir.AluOpType
ACT = mybir.ActivationFunctionType
AX = mybir.AxisListType

C_IDENT, C_CAUSAL, C_HADAMARD, C_BLOCKS, C_END = 0, P, 2 * P, 3 * P, 3 * P + HEADS * DV


def steps(text):
    return [(name, int(k)) for name, k in (word.split(".") for word in text.split())]


FIRST = steps("w_hi.0 stats.0 norm.0 stats.1 norm.1 mod.0 w_hi.1 h1.0 w_lo.0 h1lo.0 h1.1 h1lo.1 qk.0 vg.0 fly_b.0 "
              "qk.1 fly_b.1 fly_b.2 fly_a.0 rows.0 qk.2 fly_b.3 vg.1 w_o.0 mod.1 qk.3 w_w13.0 zero.0 fly_a.1 vg.2 "
              "fly_b.4 vg.3 fly_a.2 w_w13.1 ksplit.0 qt.0 kt.0 qblk.0 fly_a.3 fly_b.5 gates.0 fly_a.4 stats.2 "
              "score.0 state.0 fly_a.5 fold.0 score.1 plo.0 state.1 fold.1 score.2 plo.1 o.0 fold.2 state.2 score.3 "
              "plo.2 o.1 ss.0 plo.3 ss.1 o.2 had.0 had.1 o.3 rms.0 ss.2 ss.3 had.2 yt.0 rms.1 fold.3 w_w13.2 "
              "stats.3 stats.4 yt.1 stats.5 proj.0 proj.1 norm2.0 had.3 norm2.1 w_w13.3 h2.0 h2.1 h2lo.0 h2lo.1 "
              "stats.6 stats.7")
STEADY = steps("norm.0 up.0 h1.0 hid.0 norm.1 h1lo.0 up.1 h1.1 qk.0 h1lo.1 up.2 qk.1 hid.1 vg.0 qk.2 vg.1 vg.2 qk.3 "
               "vg.3 ksplit.0 down.0 qt.0 hid.2 kt.0 qblk.0 down.1 up.3 hid.3 score.0 state.0 down.2 plo.0 score.1 "
               "state.1 plo.1 o.0 score.2 state.2 o.1 ss.0 ss.1 down.3 score.3 plo.2 plo.3 up.4 rms.0 hid.4 o.2 ss.2 "
               "o.3 ss.3 yt.0 up.5 rms.1 proj.0 down.4 yt.1 norm2.0 up.6 hid.5 hid.6 proj.1 up.7 norm2.1 hid.7 h2.0 "
               "down.5 h2.1 h2lo.0 h2lo.1 down.6 down.7 out.0 out.1")
LAST = steps("up.0 up.1 hid.0 hid.1 up.2 up.3 down.0 up.4 hid.2 hid.3 down.1 up.5 hid.4 down.2 down.3 up.6 down.4 "
             "hid.5 hid.6 up.7 down.5 hid.7 down.6 down.7 out.0 out.1")


class Signal:

    def __init__(self, sem, per, start=0):
        self.sem, self.per, self.start = sem, per, start

    def after(self, batch, k):
        return batch * self.per + (self.start + k)


def adaln_block_kernel(nc, x, c_t, w_qkvg, w_o, gnorm, w13, w2, wmod, consts, select, cos, sin, out):
    with ExitStack() as ctx:
        def sb(name, shape, dt=F32, scope=ctx):
            return scope.enter_context(nc.sbuf_tensor(name, shape, dt))

        def bank(name):
            return ctx.enter_context(nc.psum_tensor(name, [P, 512], F32))

        def sem(name, per=0, start=0):
            return Signal(ctx.enter_context(nc.semaphore(name)), per, start)

        xres = sb("xres", [P, B, TILES, D])
        mod_cols = sb("mod_cols", [P, B, 4, KC])
        gates = sb("gates", [P, B, 2, D])
        cst = sb("cst", [P, C_END])
        ident, causal = cst[:, C_IDENT:C_IDENT + P], cst[:, C_CAUSAL:C_CAUSAL + P]
        hadamard, blocks = cst[:, C_HADAMARD:C_HADAMARD + P], cst[:, C_BLOCKS:C_END]
        had_r = sb("had_r", [P, P], F32R)
        cos_sb, sin_sb = sb("cos_sb", [P, TILES, QK]), sb("sin_sb", [P, TILES, QK])
        gnorm_in, gnorm_sb = sb("gnorm_in", [P, DV]), sb("gnorm_sb", [P, DV])
        mhalf = sb("mhalf", [P, 2 * HEADS])
        eps_ln, eps_rms = sb("eps_ln", [P, TILES]), sb("eps_rms", [P, 2 * HEADS])
        c_sb, sc_sb = sb("c_sb", [P, KC, B]), sb("sc_sb", [P, KC, B])
        mv1 = sb("mv1", [P, B, TILES, 2])
        ve1, rs1 = sb("ve1", [P, B, TILES]), sb("rs1", [P, B, TILES])
        wqkvg_hi, wqkvg_lo = (sb("wqkvg_" + e, [P, KC, QK + VG], F32R) for e in ("hi", "lo"))
        wo_hi, wo_lo = (sb("wo_" + e, [P, KC, D], F32R) for e in ("hi", "lo"))
        w13_hi, w13_lo = (sb("w13_" + e, [P, PIECES, 2, KC, PW], F32R) for e in ("hi", "lo"))

        stats1, stats = sb("stats1", [P, TILES, 6]), sb("stats", [P, TILES, 6])
        mv_cur, rs_cur = sb("mv_cur", [P, TILES, 2]), sb("rs_cur", [P, TILES])
        mod_cur = sb("mod_cur", [P, 4, KC])
        mv2, ve2, rs2 = sb("mv2", [P, TILES, 2]), sb("ve2", [P, TILES]), sb("rs2", [P, TILES])
        xn = sb("xn", [P, TILES, D])
        h32 = sb("h32", [P, KC, N])
        p32 = h32[:, :, :].rearrange("p k (h i) -> p k h i", h=HEADS)
        h1_hi, h1_lo = sb("h1_hi", [P, KC, N], F32R), sb("h1_lo", [P, KC, N], F32R)
        rope_a, rope_b = sb("rope_a", [P, 2, QK]), sb("rope_b", [P, 2, QK])
        qk = sb("qk", [P, TILES, QK])
        x1 = qk
        k_hi, k_lo = sb("k_hi", [P, TILES, P], F32R), sb("k_lo", [P, TILES, P], F32R)
        v2 = sb("v2", [P, TILES, HEADS, 2, DV], F32R)
        v_hi, v_lo = v2[:, :, :, 0, :], v2[:, :, :, 1, :]
        gg = sb("gg", [P, TILES, D])
        qt_hi, qt_lo = sb("qt_hi", [P, TILES, P], F32R), sb("qt_lo", [P, TILES, P], F32R)
        kt_hi, kt_lo = sb("kt_hi", [P, TILES, P], F32R), sb("kt_lo", [P, TILES, P], F32R)
        p_hi, p_lo = sb("p_hi", [P, 2, HEADS, P], F32R), sb("p_lo", [P, 2, HEADS, P], F32R)
        s32 = sb("s32", [P, HEADS * DV])
        s_hi, s_lo = sb("s_hi", [P, 2, HEADS * DV], F32R), sb("s_lo", [P, 2, HEADS * DV], F32R)
        sq = sb("sq", [P, 2, D])
        ss, vo, rso = (sb(n, [P, TILES, HEADS]) for n in ("ss", "vo", "rso"))
        tmp = sb("tmp", [P, 2, D])
        branch = (tmp, sq)
        unread = sb("unread", [P, 1])

        gate_row = tmp[0:B].rearrange("b g d -> b (g d)")
        gate_size = sq[0:B].rearrange("b g d -> b (g d)")

        with ExitStack() as scope:
            fly0 = sb("fly0", [P, HB, D], scope=scope)
        w2_hi = sb("w2_hi", [P, HB, D], F32R)
        w2_lo = sb("w2_lo", [P, HB, D], F32R)
        with ExitStack() as scope:
            wmod_sb = sb("wmod_sb", [P, KC, 6 * D], scope=scope)
            stage_qkvg = sb("stage_qkvg", [P, KC, QK + VG], scope=scope)
        qb_hi = sb("qb_hi", [P, TILES, HEADS, P], F32R)
        qb_lo = sb("qb_lo", [P, TILES, HEADS, P], F32R)
        g32 = sb("g32", [P, 2, D])
        with ExitStack() as scope:
            fly1 = sb("fly1", [P, HB, D], scope=scope)
            stage_13 = sb("stage_13", [P, 2, 2, KC, PW], scope=scope)
            stage_wo = sb("stage_wo", [P, KC, D], scope=scope)
            sel_sb = sb("sel_sb", [B, B, P], scope=scope)
        h2_hi, h2_lo = sb("h2_hi", [P, KC, N], F32R), sb("h2_lo", [P, KC, N], F32R)
        silu1, hid32 = sb("silu1", [P, 2, N]), sb("hid32", [P, 2, N])
        hid_hi, hid_lo = sb("hid_hi", [P, 2, N], F32R), sb("hid_lo", [P, 2, N], F32R)

        pa, pb, pc, pstate = bank("pa"), bank("pb"), bank("pc"), bank("pstate")
        pu1, pu3, pacc0, pacc1 = bank("pu1"), bank("pu3"), bank("pacc0"), bank("pacc1")
        ph1, pvg, po, py, pw, ph2 = (pa, pb), (pc, pb), (pa, pb), (pc, pb), (pa, pc), (pb, pa)
        pacc, pffn = (pacc0, pacc1), (pu1, pu3, pacc0, pacc1)

        in_xr, in_c, in_cst, in_mod1, in_mod2, in_wqkvg, in_wo, in_w2, in_cos, in_sin, in_gn, in_sel = (
            sem("in_" + n) for n in "xr c cst mod1 mod2 wqkvg wo w2 cos sin gn sel".split())
        in_x0 = [sem(f"in_x0_{n}") for n in range(2)]
        in_w13 = [sem(f"in_w13_{i}") for i in range(PIECES)]
        a_sc, a_gn, a_wqkvg, d_wqkvg, p_wqkvg, a_wo, d_wo_lo, a_w13, d_w13, p_w13 = (
            sem(n) for n in "a_sc a_gn a_wqkvg d_wqkvg p_wqkvg a_wo d_wo_lo a_w13 d_w13 p_w13".split())
        t_cols1, t_cols2, t_rows, t_gates, d_cols1, d_cols2, d_rows, a_gates = (
            sem(n) for n in "t_cols1 t_cols2 t_rows t_gates d_cols1 d_cols2 d_rows a_gates".split())
        d_st1, d_mv1, p_ve1, p_rs1, p_mhalf, p_zero = (
            sem(n) for n in "d_st1 d_mv1 p_ve1 p_rs1 p_mhalf p_zero".split())
        p_fly, a_had, a_fly, d_flya, p_w2lo, t_had, a_w2, d_w2 = (
            sem(n) for n in "p_fly a_had a_fly d_flya p_w2lo t_had a_w2 d_w2".split())
        d_cur = sem("d_cur", 1, start=1)
        d_cur1, d_qb, a_qb, a_k, p_k = (
            sem(n, 1) for n in "d_cur1 d_qb a_qb a_k p_k".split())
        d_xn1, t_xn1, d_h1, a_h1, d_h1lo, t_qkt, a_qkt, d_qkt = (
            sem(n, 2) for n in "d_xn1 t_xn1 d_h1 a_h1 d_h1lo t_qkt a_qkt d_qkt".split())
        t_qk, t_vg, d_rope, p_rope, a_vg, d_vlo, p_gg = (
            sem(n, TILES) for n in "t_qk t_vg d_rope p_rope a_vg d_vlo p_gg".split())
        t_s, d_p, a_p, d_plo, t_o, a_o, d_o, a_sq, p_y0, d_ss = (
            sem(n, TILES) for n in "t_s d_p a_p d_plo t_o a_o d_o a_sq p_y0 d_ss".split())
        t_kv, d_s, a_s, p_s = (sem(n, TILES - 1) for n in "t_kv d_s a_s p_s".split())
        t_yt, a_yt, d_yt, t_wo, d_wo, d_x1, d_st2, d_mv2, p_ve2, p_rs2 = (
            sem(n, 2) for n in "t_yt a_yt d_yt t_wo d_wo d_x1 d_st2 d_mv2 p_ve2 p_rs2".split())
        d_cur2, d_xn2, t_xn2, d_h2, a_h2, d_h2lo, p_vo, p_rso, d_y = (
            sem(n, 2) for n in "d_cur2 d_xn2 t_xn2 d_h2 a_h2 d_h2lo p_vo p_rso d_y".split())
        t_u1, t_u3, a_silu, d_hid, a_hid, p_hid = (
            sem(n, HB) for n in "t_u1 t_u3 a_silu d_hid a_hid p_hid".split())
        t_d, d_lastlo = sem("t_d", HB - 1), sem("d_lastlo")
        t_acc, d_fin, stored = sem("t_acc", 2), sem("d_fin", 2), sem("stored", 2 * 16)
        p_x1, p_out = sem("p_x1", 2), sem("p_out", 2, start=1)

        def heads(columns):
            return columns.rearrange("p (h v) -> p h v", h=HEADS)

        def very_last(f, k):
            return isinstance(f, int) and k == HB - 1

        def butterfly(engine, k, parts, done):
            stage, n = divmod(k, len(parts))
            cols = slice(parts[n] * D // PARTS, (parts[n] + 1) * D // PARTS)
            if k == 0:
                engine.wait_ge(in_w2.sem, 16)
            if stage:
                engine.wait_ge(done.sem, k - len(parts) + 1)
            src, dst = (t[:, :, cols].rearrange("p (g s r) d -> p g s r d", s=2, r=2 ** stage)
                        for t in ((fly0, fly1), (fly1, fly0))[stage % 2])
            engine.tensor_tensor(dst[:, :, 0], src[:, :, 0], src[:, :, 1], ALU.add)
            engine.tensor_tensor(dst[:, :, 1], src[:, :, 0], src[:, :, 1], ALU.subtract).then_inc(done.sem, 1)

        def run(engine, step):
            for kind, k in FIRST:
                step(kind, k, 0, None)
            with engine.Fori(1, B) as b:
                for kind, k in STEADY:
                    step(kind, k, b, b - 1)
            for kind, k in LAST:
                step(kind, k, None, B - 1)

        block = ctx.enter_context(nc.Block())

        @block.sync
        def _(sp):
            sp.dma_start(c_sb[:], c_t).then_inc(in_c.sem, 16)
            for n in range(2):
                sp.dma_start(xres[:, 0, 2 * n:2 * n + 2], x[0, 2 * n * P:(2 * n + 2) * P].rearrange(
                    "(t p) d -> p t d", p=P)).then_inc(in_x0[n].sem, 16)
            sp.dma_start(wmod_sb[:, :, 0:2 * D], wmod[:, :, 0:2 * D]).then_inc(in_mod1.sem, 16)
            sp.dma_start(cst[:], consts).then_inc(in_cst.sem, 16)
            sp.dma_start(stage_qkvg[:], w_qkvg).then_inc(in_wqkvg.sem, 16)
            sp.dma_start(cos_sb[:], cos).then_inc(in_cos.sem, 16)
            sp.dma_start(sin_sb[:], sin).then_inc(in_sin.sem, 16)
            sp.dma_start(gnorm_in[:], gnorm).then_inc(in_gn.sem, 16)
            sp.dma_start(wmod_sb[:, :, 2 * D:6 * D], wmod[:, :, 2 * D:6 * D]).then_inc(in_mod2.sem, 16)
            sp.dma_start(sel_sb[:], select).then_inc(in_sel.sem, 16)
            sp.dma_start(fly0[:], w2).then_inc(in_w2.sem, 16)
            sp.dma_start(stage_wo[:], w_o).then_inc(in_wo.sem, 16)
            for i in range(PIECES):
                if i == 2:
                    sp.dma_start(xres[:, 1:B], x[1:B].rearrange("b (t p) d -> p (b t) d", p=P)
                                 ).then_inc(in_xr.sem, 16)
                if i >= 2:
                    sp.wait_ge(d_w13.sem, i - 1)
                sp.dma_start(stage_13[:, i % 2], w13[i]).then_inc(in_w13[i].sem, 16)

            def store(f):
                for n in range(2):
                    sp.wait_ge(p_out.sem, p_out.after(f, n + 1))
                    sp.dma_start(out[f, 2 * n * P:(2 * n + 2) * P].rearrange("(t p) d -> p t d", p=P),
                                 xres[:, f, 2 * n:2 * n + 2]).then_inc(stored.sem, 16)

            with sp.Fori(1, B) as b:
                store(b - 1)
            store(B - 1)
            sp.wait_ge(stored.sem, stored.after(B, 0))

        @block.tensor
        def _(pe):
            def three(ps, parts, start=True, stop=True):
                ops = [(a, c) for (ah, al), (ch, cl) in parts for a, c in ((ah, ch), (ah, cl), (al, ch))]
                for n, (a, c) in enumerate(ops):
                    mm = pe.matmul(ps, a, c, start=start and n == 0, stop=stop and n == len(ops) - 1,
                                   skip_group_check=True)
                return mm

            def columns(parts, at, done):
                for part in parts:
                    for h in range(KC):
                        col = part * D + h * P
                        for kc in range(KC):
                            mm = pe.matmul(pu1[:, at:at + B], wmod_sb[:, kc, col:col + P], sc_sb[:, kc, :],
                                           start=(kc == 0), stop=(kc == KC - 1))
                        at += B
                mm.then_inc(done.sem, 1)

            def step(kind, k, b, f):
                first = b == 0 if isinstance(b, int) else False
                if kind == "mod" and k == 0:
                    pe.wait_ge(in_mod1.sem, 16)
                    pe.wait_ge(a_sc.sem, 1)
                    columns((SA, CA), 0, t_cols1)
                elif kind == "mod":
                    pe.wait_ge(in_mod2.sem, 16)
                    pe.wait_ge(d_cols1.sem, 1)
                    columns((SB, CB), 2 * KC * B, t_cols2)
                elif kind == "rows":
                    pe.wait_ge(in_mod2.sem, 16)
                    for n, part in enumerate((GA, GB)):
                        for kc in range(KC):
                            mm = pe.matmul(pu3[0:B, n * D:(n + 1) * D], sc_sb[:, kc, :],
                                           wmod_sb[:, kc, part * D:(part + 1) * D],
                                           start=(kc == 0), stop=(kc == KC - 1))
                    mm.then_inc(t_rows.sem, 1)
                elif kind == "gates":
                    pe.wait_ge(in_sel.sem, 16)
                    pe.wait_ge(d_cols2.sem, 1)
                    pe.wait_ge(d_rows.sem, 4)
                    for n in range(B):
                        pe.matmul(pffn[n][:, :], sel_sb[:, n, :], gate_row,
                                  start=True, stop=True).then_inc(t_gates.sem, 1)
                elif kind == "h1":
                    if first and k == 0:
                        pe.wait_ge(in_cst.sem, 16)
                    pe.wait_ge(d_xn1.sem, d_xn1.after(b, k + 1))
                    for kc in range(KC):
                        for j in range(2):
                            mm = pe.transpose(ph1[k][:, (2 * kc + j) * P:(2 * kc + j + 1) * P],
                                              xn[:, 2 * k + j, kc * P:(kc + 1) * P], ident)
                    mm.then_inc(t_xn1.sem, 1)
                elif kind == "qk":
                    if k == 0 and first:
                        pe.wait_ge(d_wqkvg.sem, 1)
                        pe.wait_ge(p_wqkvg.sem, 1)
                    if k % 2 == 0:
                        pe.wait_ge(d_h1lo.sem, d_h1lo.after(b, k // 2 + 1))
                    if k:
                        pe.wait_ge(d_rope.sem, d_rope.after(b, k))
                    tok = slice(k * P, (k + 1) * P)
                    three(pa[:, 0:QK], [((h1_hi[:, kc, tok], h1_lo[:, kc, tok]),
                                         (wqkvg_hi[:, kc, 0:QK], wqkvg_lo[:, kc, 0:QK])) for kc in range(KC)]
                          ).then_inc(t_qk.sem, 1)
                elif kind == "vg":
                    if k == 1:
                        pe.wait_ge(d_h1.sem, d_h1.after(b, 2))
                    elif k >= 2:
                        pe.wait_ge(d_vlo.sem, d_vlo.after(b, k - 1))
                    tok = slice(k * P, (k + 1) * P)
                    three(pvg[k % 2][:, :], [((h1_hi[:, kc, tok], h1_lo[:, kc, tok]),
                                              (wqkvg_hi[:, kc, QK:QK + VG], wqkvg_lo[:, kc, QK:QK + VG]))
                                             for kc in range(KC)]).then_inc(t_vg.sem, 1)
                elif kind == "qt":
                    pe.wait_ge(p_rope.sem, p_rope.after(b, TILES))
                    for t in range(TILES):
                        mm = pe.transpose(pa[:, t * P:(t + 1) * P], qk[:, t, 0:P], ident)
                    mm.then_inc(t_qkt.sem, 1)
                elif kind == "kt":
                    pe.wait_ge(d_vlo.sem, d_vlo.after(b, TILES))
                    for t in range(TILES):
                        mm = pe.transpose(pb[:, t * P:(t + 1) * P], qk[:, t, P:2 * P], ident)
                    mm.then_inc(t_qkt.sem, 1)
                elif kind == "score":
                    if k == 0:
                        pe.wait_ge(d_qb.sem, d_qb.after(b, 1))
                        pe.wait_ge(a_qb.sem, a_qb.after(b, 1))
                    else:
                        pe.wait_ge(d_p.sem, d_p.after(b, k))
                    three(pc[:, :], [((kt_hi[:, k], kt_lo[:, k]), (qb_hi[:, k], qb_lo[:, k]))]
                          ).then_inc(t_s.sem, 1)
                elif kind == "state":
                    if k == 0:
                        pe.wait_ge(p_k.sem, p_k.after(b, 1))
                    else:
                        pe.wait_ge(d_s.sem, d_s.after(b, k))
                    three(pstate[:, 0:HEADS * DV], [((k_hi[:, k], k_lo[:, k]), (v_hi[:, k], v_lo[:, k]))],
                          start=(k == 0)).then_inc(t_kv.sem, 1)
                elif kind == "o":
                    if k >= 2:
                        pe.wait_ge(d_o.sem, d_o.after(b, k - 1))
                    out_k = po[k % 2][:, :].rearrange("p (h s v) -> p h s v", h=HEADS, s=2)
                    if k:
                        pe.wait_ge(p_s.sem, p_s.after(b, k))
                        three(out_k[:, :, 0], [((qt_hi[:, k], qt_lo[:, k]),
                                                (s_hi[:, (k - 1) % 2], s_lo[:, (k - 1) % 2]))], stop=False)
                    pe.wait_ge(d_plo.sem, d_plo.after(b, k + 1))
                    for h in range(HEADS):
                        pe.matmul(out_k[:, h], p_hi[:, k % 2, h], v2[:, k, h], start=(k == 0 and h == 0), stop=False,
                                  skip_group_check=True)
                        mm = pe.matmul(out_k[:, h, 0], p_lo[:, k % 2, h], v2[:, k, h, 0], start=False,
                                       stop=(h == HEADS - 1), skip_group_check=True)
                    mm.then_inc(t_o.sem, 1)
                elif kind == "yt":
                    pe.wait_ge(d_y.sem, d_y.after(b, k + 1))
                    for kc in range(KC):
                        for j in range(2):
                            mm = pe.transpose(py[k][:, (2 * kc + j) * P:(2 * kc + j + 1) * P],
                                              xn[:, 2 * k + j, kc * P:(kc + 1) * P], ident)
                    mm.then_inc(t_yt.sem, 1)
                elif kind == "proj":
                    pe.wait_ge(d_yt.sem, d_yt.after(b, k + 1))
                    if k == 0:
                        pe.wait_ge(d_o.sem, d_o.after(b, 3))
                        if first:
                            pe.wait_ge(d_wo_lo.sem, 1)
                    for j in range(2):
                        tok = slice((2 * k + j) * P, (2 * k + j + 1) * P)
                        mm = three(pw[k][:, j * D:(j + 1) * D],
                                   [((h1_hi[:, kc, tok], h1_lo[:, kc, tok]), (wo_hi[:, kc], wo_lo[:, kc]))
                                    for kc in range(KC)])
                    mm.then_inc(t_wo.sem, 1)
                elif kind == "h2":
                    pe.wait_ge(d_xn2.sem, d_xn2.after(b, k + 1))
                    for kc in range(KC):
                        for j in range(2):
                            mm = pe.transpose(ph2[k][:, (2 * kc + j) * P:(2 * kc + j + 1) * P],
                                              xn[:, 2 * k + j, kc * P:(kc + 1) * P], ident)
                    mm.then_inc(t_xn2.sem, 1)
                elif kind == "had":
                    if k == 0:
                        pe.wait_ge(a_gates.sem, B)
                        pe.wait_ge(a_had.sem, 1)
                    pe.wait_ge(p_w2lo.sem, k + 1)
                    pe.matmul(pffn[k][:, :], had_r[:], w2_hi[:, 2 * k:2 * k + 2, :], start=True, stop=False)
                    pe.matmul(pffn[k][:, :], had_r[:], w2_lo[:, 2 * k:2 * k + 2, :], start=False, stop=True
                              ).then_inc(t_had.sem, 1)
                elif kind == "up":
                    if k == 0:
                        pe.wait_ge(d_h2lo.sem, d_h2lo.after(f, KC))
                        pe.wait_ge(d_w2.sem, len(pffn))
                        pe.wait_ge(d_w13.sem, len(W13_A))
                        pe.wait_ge(p_w13.sem, len(W13_B))
                    piece, col = divmod(k * P, PW)
                    for w, ps, read, done in ((0, pu1, a_silu, t_u1), (1, pu3, d_hid, t_u3)):
                        if k:
                            pe.wait_ge(read.sem, read.after(f, k))
                        three(ps[:, :], [((w13_hi[:, piece, w, kc, col:col + P],
                                           w13_lo[:, piece, w, kc, col:col + P]),
                                          (h2_hi[:, kc], h2_lo[:, kc])) for kc in range(KC)]
                              ).then_inc(done.sem, 1)
                elif kind == "down":
                    if k == 0 and isinstance(f, int):
                        pe.wait_ge(d_fin.sem, d_fin.after(f, 0))
                    if very_last(f, k):
                        pe.wait_ge(d_lastlo.sem, 1)
                    else:
                        pe.wait_ge(p_hid.sem, p_hid.after(f, k + 1))
                    for t in range(TILES):
                        tok = slice(t * P, (t + 1) * P)
                        mm = three(pacc[t // 2][:, t % 2 * D:(t % 2 + 1) * D],
                                   [((hid_hi[:, k % 2, tok], hid_lo[:, k % 2, tok]), (w2_hi[:, k], w2_lo[:, k]))],
                                   start=(k == 0 and t % 2 == 0), stop=(k == HB - 1))
                        if k == HB - 1 and t % 2:
                            mm.then_inc(t_acc.sem, 1)
                    if k < HB - 1:
                        mm.then_inc(t_d.sem, 1)

            run(pe, step)

        @block.vector
        def _(dve):
            def step(kind, k, b, f):
                first = b == 0 if isinstance(b, int) else False
                if kind == "stats":
                    m, n = divmod(k, 2)
                    dve.wait_ge((in_xr if m else in_x0[n]).sem, 16)
                    if m:
                        dve.wait_ge(d_mv1.sem, k - 1)
                    for t in (2 * n, 2 * n + 1):
                        ins = dve.bn_stats(stats1[:, t, :], xres[:, m, t])
                    ins.then_inc(d_st1.sem, 1)
                    dve.wait_ge(d_st1.sem, k + 1)
                    for t in (2 * n, 2 * n + 1):
                        ins = dve.bn_aggr(mv1[:, m, t], stats1[:, t, :])
                    ins.then_inc(d_mv1.sem, 1)
                elif kind == "mod" and k == 0:
                    dve.wait_ge(t_cols1.sem, 1)
                    for n, add in ((0, 0.0), (1, 1.0)):
                        ins = dve.tensor_scalar(mod_cols[:, :, n, :], pu1[:, n * KC * B:(n + 1) * KC * B].rearrange(
                            "p (h b) -> p b h", b=B), add, None, ALU.add)
                    ins.then_inc(d_cols1.sem, 1)
                elif kind == "mod":
                    dve.wait_ge(t_cols2.sem, 1)
                    for n, add in ((2, 0.0), (3, 1.0)):
                        ins = dve.tensor_scalar(mod_cols[:, :, n, :], pu1[:, n * KC * B:(n + 1) * KC * B].rearrange(
                            "p (h b) -> p b h", b=B), add, None, ALU.add)
                    ins.then_inc(d_cols2.sem, 1)
                elif kind == "rows":
                    dve.wait_ge(t_rows.sem, 1)
                    dve.tensor_scalar(gate_row, pu3[0:B, :], 0.0, 2.0, ALU.is_ge, ALU.mult
                                      ).then_inc(d_rows.sem, 1)
                    dve.wait_ge(d_rows.sem, 1)
                    dve.scalar_tensor_tensor(out=gate_size, in0=gate_row, scalar=-1.0, in1=pu3[0:B, :],
                                             op0=ALU.add, op1=ALU.mult).then_inc(d_rows.sem, 1)
                    dve.wait_ge(d_rows.sem, 2)
                    dve.tensor_scalar(gate_size, gate_size, MIN_GATE, None, ALU.max).then_inc(d_rows.sem, 1)
                    dve.wait_ge(d_rows.sem, 3)
                    dve.scalar_tensor_tensor(out=gate_row, in0=gate_row, scalar=-1.0, in1=gate_size,
                                             op0=ALU.add, op1=ALU.mult).then_inc(d_rows.sem, 1)
                elif kind == "w_lo":
                    dve.wait_ge(a_wqkvg.sem, 2)
                    dve.tensor_tensor(wqkvg_lo[:, 1], stage_qkvg[:, 1], wqkvg_hi[:, 1].bitcast(F32), ALU.subtract
                                      ).then_inc(d_wqkvg.sem, 1)
                elif kind == "w_o":
                    dve.wait_ge(a_wo.sem, 1)
                    dve.tensor_tensor(wo_lo[:], stage_wo[:], wo_hi[:].bitcast(F32), ALU.subtract
                                      ).then_inc(d_wo_lo.sem, 1)
                elif kind == "w_w13" and k in W13_A:
                    dve.wait_ge(a_w13.sem, k + 1)
                    dve.tensor_tensor(w13_lo[:, k], stage_13[:, k % 2], w13_hi[:, k].bitcast(F32), ALU.subtract
                                      ).then_inc(d_w13.sem, 1)
                elif kind == "fly_a":
                    butterfly(dve, k, FLY_A, d_flya)
                elif kind == "had":
                    dve.wait_ge(a_w2.sem, k + 1)
                    dve.scalar_tensor_tensor(out=w2_lo[:, 2 * k:2 * k + 2, :], in0=pffn[k][:, :].rearrange(
                        "p (n d) -> p n d", n=2), scalar=HID ** -0.5,
                        in1=w2_hi[:, 2 * k:2 * k + 2, :].bitcast(F32), op0=ALU.mult, op1=ALU.subtract
                        ).then_inc(d_w2.sem, 1)
                elif kind == "norm":
                    pair = slice(2 * k, 2 * k + 2)
                    if first:
                        dve.wait_ge(p_rs1.sem, k + 1)
                        dve.wait_ge(d_mv1.sem, k + 1)
                    elif k == 0:
                        dve.wait_ge(p_rs1.sem, 2 * B)
                        dve.wait_ge(d_mv1.sem, 2 * B)
                    if first or k == 0:
                        now = pair if first else slice(0, TILES)
                        dve.tensor_copy(rs_cur[:, now], rs1[:, b, now])
                        dve.tensor_copy(mv_cur[:, now], mv1[:, b, now]).then_inc(d_cur.sem, 1)
                    dve.wait_ge(d_cur.sem, d_cur.after(b, 1) if not first else k + 1)
                    for t in (2 * k, 2 * k + 1):
                        ins = dve.tensor_scalar(xn[:, t], xres[:, b, t], mv_cur[:, t, 0:1], rs_cur[:, t:t + 1],
                                                ALU.subtract, ALU.mult)
                    ins.then_inc(d_xn1.sem, 1)
                elif kind == "h1":
                    if k == 0:
                        if first:
                            dve.wait_ge(d_cols1.sem, 1)
                        dve.tensor_copy(mod_cur[:, 0:2], mod_cols[:, b, 0:2]).then_inc(d_cur1.sem, 1)
                        dve.wait_ge(d_cur1.sem, d_cur1.after(b, 1))
                    dve.wait_ge(t_xn1.sem, t_xn1.after(b, k + 1))
                    for kc in range(KC):
                        ins = dve.tensor_scalar(h32[:, kc, 2 * k * P:(2 * k + 2) * P],
                                                ph1[k][:, 2 * kc * P:(2 * kc + 2) * P], mod_cur[:, 1, kc:kc + 1],
                                                mod_cur[:, 0, kc:kc + 1], ALU.mult, ALU.add)
                    ins.then_inc(d_h1.sem, 1)
                elif kind == "h1lo":
                    tok = slice(2 * k * P, (2 * k + 2) * P)
                    dve.wait_ge(a_h1.sem, a_h1.after(b, k + 1))
                    dve.tensor_tensor(h1_lo[:, :, tok], h32[:, :, tok], h1_hi[:, :, tok].bitcast(F32), ALU.subtract
                                      ).then_inc(d_h1lo.sem, 1)
                elif kind == "qk":
                    if first and k == 0:
                        dve.wait_ge(in_cos.sem, 16)
                        dve.wait_ge(in_sin.sem, 16)
                    dve.wait_ge(t_qk.sem, t_qk.after(b, k + 1))
                    if k >= 2 or not first:
                        dve.wait_ge(p_rope.sem, p_rope.after(b, k - 1))
                    dve.tensor_tensor(rope_a[:, k % 2], pa[:, 0:QK], cos_sb[:, k], ALU.mult)
                    halves = [t.rearrange("p (g s e) -> p g s e", s=2, e=DK // 2)
                              for t in (rope_b[:, k % 2], pa[:, 0:QK], sin_sb[:, k])]
                    for s in range(2):
                        ins = dve.tensor_tensor(halves[0][:, :, 1 - s], halves[1][:, :, s], halves[2][:, :, s],
                                                ALU.mult)
                    ins.then_inc(d_rope.sem, 1)
                elif kind == "vg":
                    dve.wait_ge(a_vg.sem, a_vg.after(b, k + 1))
                    dve.tensor_tensor(v_lo[:, k], heads(pvg[k % 2][:, 0:D]), v_hi[:, k].bitcast(F32), ALU.subtract
                                      ).then_inc(d_vlo.sem, 1)
                elif kind in ("qt", "kt"):
                    n, ps, hi, lo = (0, pa, qt_hi, qt_lo) if kind == "qt" else (1, pb, kt_hi, kt_lo)
                    dve.wait_ge(a_qkt.sem, a_qkt.after(b, n + 1))
                    dve.tensor_tensor(lo[:], ps[:, :].rearrange("p (t i) -> p t i", t=TILES),
                                      hi[:].bitcast(F32), ALU.subtract).then_inc(d_qkt.sem, 1)
                elif kind == "qblk":
                    if first:
                        dve.wait_ge(p_zero.sem, 2)
                    dve.wait_ge(d_qkt.sem, d_qkt.after(b, 1))
                    for h in range(HEADS):
                        rows = slice(h * DK, (h + 1) * DK)
                        ins = dve.tensor_copy(qb_lo[rows, :, h, :], qt_lo[rows].bitcast(F32))
                    ins.then_inc(d_qb.sem, 1)
                elif kind == "score":
                    if k >= 2:
                        dve.wait_ge(d_plo.sem, d_plo.after(b, k - 1))
                    dve.wait_ge(t_s.sem, t_s.after(b, k + 1))
                    dve.tensor_tensor(p32[:, k % 2], pc[:, :].rearrange("p (h i) -> p h i", h=HEADS),
                                      causal.unsqueeze(1).to_broadcast([P, HEADS, P]), ALU.mult
                                      ).then_inc(d_p.sem, 1)
                elif kind == "plo":
                    dve.wait_ge(a_p.sem, a_p.after(b, k + 1))
                    dve.tensor_tensor(p_lo[:, k % 2], p32[:, k % 2], p_hi[:, k % 2].bitcast(F32), ALU.subtract
                                      ).then_inc(d_plo.sem, 1)
                elif kind == "state":
                    dve.wait_ge(t_kv.sem, t_kv.after(b, k + 1))
                    if k:
                        dve.wait_ge(p_s.sem, p_s.after(b, k))
                    dve.tensor_tensor(s32[:], pstate[:, 0:HEADS * DV], blocks, ALU.mult).then_inc(d_s.sem, 1)
                elif kind == "o":
                    dve.wait_ge(a_o.sem, a_o.after(b, k + 1))
                    parts = po[k % 2][:, :].rearrange("p (h s v) -> p h s v", h=HEADS, s=2)
                    dve.tensor_tensor(heads(xn[:, k]), parts[:, :, 0], heads(xn[:, k]), ALU.add).then_inc(d_o.sem, 1)
                elif kind == "ss":
                    dve.wait_ge(a_sq.sem, a_sq.after(b, k + 1))
                    dve.reduce_sum(ss[:, k], heads(sq[:, k % 2]), AX.X).then_inc(d_ss.sem, 1)
                elif kind == "rms":
                    dve.wait_ge(p_rso.sem, p_rso.after(b, k + 1))
                    pair = slice(2 * k, 2 * k + 2)
                    y = xn[:, pair].rearrange("p t (h v) -> p (t h) v", h=HEADS)
                    dve.wait_ge(p_y0.sem, p_y0.after(b, 2 * k + 2))
                    dve.tensor_tensor(y, y, rso[:, pair].rearrange("p t h -> p (t h)").unsqueeze(2).to_broadcast(
                        [P, 2 * HEADS, DV]), ALU.mult).then_inc(d_y.sem, 1)
                elif kind == "yt":
                    dve.wait_ge(a_yt.sem, a_yt.after(b, k + 1))
                    tok = slice(2 * k * P, (2 * k + 2) * P)
                    dve.tensor_tensor(h1_lo[:, :, tok], py[k][:, :].rearrange("p (k n) -> p k n", k=KC),
                                      h1_hi[:, :, tok].bitcast(F32), ALU.subtract).then_inc(d_yt.sem, 1)
                elif kind == "proj":
                    dve.wait_ge(t_wo.sem, t_wo.after(b, k + 1))
                    if first and k == 0:
                        dve.wait_ge(a_gates.sem, B)
                    pair = slice(2 * k, 2 * k + 2)
                    dve.tensor_tensor(branch[k][:], pw[k][:, :].rearrange("p (t d) -> p t d", t=2),
                                      gates[:, b, 0].unsqueeze(1).to_broadcast([P, 2, D]), ALU.mult
                                      ).then_inc(d_wo.sem, 1)
                    dve.wait_ge(d_wo.sem, d_wo.after(b, k + 1))
                    dve.tensor_tensor(x1[:, pair], xres[:, b, pair], branch[k][:], ALU.add).then_inc(d_x1.sem, 1)
                    dve.wait_ge(d_x1.sem, d_x1.after(b, k + 1))
                    for t in (2 * k, 2 * k + 1):
                        ins = dve.bn_stats(stats[:, t, :], x1[:, t])
                    ins.then_inc(d_st2.sem, 1)
                    dve.wait_ge(d_st2.sem, d_st2.after(b, k + 1))
                    if first and k == 0:
                        dve.wait_ge(d_cols2.sem, 1)
                    dve.tensor_scalar(mod_cur[:, 2 + k], mod_cols[:, b, 2 + k], 1.0, None, ALU.mult
                                      ).then_inc(d_cur2.sem, 1)
                    for t in (2 * k, 2 * k + 1):
                        ins = dve.bn_aggr(mv2[:, t], stats[:, t, :])
                    ins.then_inc(d_mv2.sem, 1)
                elif kind == "norm2":
                    dve.wait_ge(p_rs2.sem, p_rs2.after(b, k + 1))
                    for t in (2 * k, 2 * k + 1):
                        ins = dve.tensor_scalar(xn[:, t], x1[:, t], mv2[:, t, 0:1], rs2[:, t:t + 1],
                                                ALU.subtract, ALU.mult)
                    ins.then_inc(d_xn2.sem, 1)
                elif kind == "h2":
                    if k == 0:
                        dve.wait_ge(d_cur2.sem, d_cur2.after(b, 2))
                    dve.wait_ge(t_xn2.sem, t_xn2.after(b, k + 1))
                    for kc in range(KC):
                        ins = dve.tensor_scalar(h32[:, kc, 2 * k * P:(2 * k + 2) * P],
                                                ph2[k][:, 2 * kc * P:(2 * kc + 2) * P], mod_cur[:, 3, kc:kc + 1],
                                                mod_cur[:, 2, kc:kc + 1], ALU.mult, ALU.add)
                    ins.then_inc(d_h2.sem, 1)
                elif kind == "h2lo":
                    tok = slice(2 * k * P, (2 * k + 2) * P)
                    dve.wait_ge(a_h2.sem, a_h2.after(b, k + 1))
                    dve.tensor_tensor(h2_lo[:, :, tok], h32[:, :, tok], h2_hi[:, :, tok].bitcast(F32), ALU.subtract
                                      ).then_inc(d_h2lo.sem, 1)
                elif kind == "up":
                    dve.wait_ge(t_u3.sem, t_u3.after(f, k + 1))
                    dve.wait_ge(a_silu.sem, a_silu.after(f, k + 1))
                    if k >= 2:
                        dve.wait_ge(p_hid.sem, p_hid.after(f, k - 1))
                    else:
                        dve.wait_ge(p_out.sem, p_out.after(f, 0))
                    dve.tensor_tensor(hid32[:, k % 2], silu1[:, k % 2], pu3[:, :], ALU.mult
                                      ).then_inc(d_hid.sem, 1)
                elif kind == "hid" and very_last(f, k):
                    dve.wait_ge(a_hid.sem, a_hid.after(f, HB))
                    dve.tensor_tensor(hid_lo[:, k % 2], hid32[:, k % 2], hid_hi[:, k % 2].bitcast(F32),
                                      ALU.subtract).then_inc(d_lastlo.sem, 1)
                elif kind == "out":
                    dve.wait_ge(t_acc.sem, t_acc.after(f, k + 1))
                    dve.tensor_tensor(hid32[:, k].rearrange("p (t d) -> p t d", t=2),
                                      pacc[k][:, :].rearrange("p (t d) -> p t d", t=2),
                                      gates[:, f, 1].unsqueeze(1).to_broadcast([P, 2, D]), ALU.mult
                                      ).then_inc(d_fin.sem, 1)

            run(dve, step)

        @block.scalar
        def _(act):
            act.wait_ge(in_c.sem, 16)
            act.activation(sc_sb[:], c_sb[:], ACT.Silu).then_inc(a_sc.sem, 1)

            def step(kind, k, b, f):
                first = b == 0 if isinstance(b, int) else False
                if kind == "w_hi":
                    if k == 0:
                        act.wait_ge(in_wqkvg.sem, 16)
                    act.activation(wqkvg_hi[:, k], stage_qkvg[:, k], ACT.Copy).then_inc(a_wqkvg.sem, 1)
                    if k == 1:
                        act.wait_ge(in_cst.sem, 16)
                        act.activation(had_r[:], hadamard, ACT.Copy).then_inc(a_had.sem, 1)
                elif kind == "w_o":
                    act.wait_ge(in_wo.sem, 16)
                    act.activation(wo_hi[:], stage_wo[:], ACT.Copy).then_inc(a_wo.sem, 1)
                elif kind == "w_w13":
                    act.wait_ge(in_w13[k].sem, 16)
                    act.activation(w13_hi[:, k], stage_13[:, k % 2], ACT.Copy).then_inc(a_w13.sem, 1)
                elif kind == "gates":
                    for n in range(B):
                        act.wait_ge(t_gates.sem, n + 1)
                        act.activation(gates[:, n].rearrange("p g d -> p (g d)"), pffn[n][:, :], ACT.Copy
                                       ).then_inc(a_gates.sem, 1)
                elif kind == "fold":
                    if k == 0:
                        act.wait_ge(d_flya.sem, STAGES * len(FLY_A))
                        act.wait_ge(p_fly.sem, STAGES * len(FLY_B))
                    act.activation(w2_hi[:, 2 * k:2 * k + 2], fly1[:, 2 * k:2 * k + 2], ACT.Copy).then_inc(a_fly.sem, 1)
                elif kind == "had":
                    act.wait_ge(t_had.sem, k + 1)
                    act.activation(w2_hi[:, 2 * k:2 * k + 2, :], pffn[k][:, :].rearrange("p (n d) -> p n d", n=2),
                                   ACT.Copy, scale=HID ** -0.5).then_inc(a_w2.sem, 1)
                elif kind == "h1":
                    tok = slice(2 * k * P, (2 * k + 2) * P)
                    act.wait_ge(d_h1.sem, d_h1.after(b, k + 1))
                    act.activation(h1_hi[:, :, tok], h32[:, :, tok], ACT.Copy).then_inc(a_h1.sem, 1)
                elif kind == "vg":
                    if first and k == 0:
                        act.wait_ge(in_gn.sem, 16)
                        act.activation(gnorm_sb[:], gnorm_in[:], ACT.Copy, scale=DV ** 0.5).then_inc(a_gn.sem, 1)
                    act.wait_ge(t_vg.sem, t_vg.after(b, k + 1))
                    act.activation(v_hi[:, k], heads(pvg[k % 2][:, 0:D]), ACT.Copy)
                    if k >= 2:
                        act.wait_ge(p_gg.sem, p_gg.after(b, k - 1))
                    act.activation(g32[:, k % 2], pvg[k % 2][:, D:2 * D], ACT.Silu).then_inc(a_vg.sem, 1)
                elif kind in ("qt", "kt"):
                    n, ps, hi = (0, pa, qt_hi) if kind == "qt" else (1, pb, kt_hi)
                    act.wait_ge(t_qkt.sem, t_qkt.after(b, n + 1))
                    act.activation(hi[:], ps[:, :].rearrange("p (t i) -> p t i", t=TILES), ACT.Copy
                                   ).then_inc(a_qkt.sem, 1)
                elif kind == "ksplit":
                    act.wait_ge(p_rope.sem, p_rope.after(b, TILES))
                    act.activation(k_hi[:], qk[:, :, P:2 * P], ACT.Copy).then_inc(a_k.sem, 1)
                elif kind == "qblk":
                    if first:
                        act.wait_ge(p_zero.sem, 2)
                    act.wait_ge(a_qkt.sem, a_qkt.after(b, 1))
                    for h in range(HEADS):
                        rows = slice(h * DK, (h + 1) * DK)
                        ins = act.activation(qb_hi[rows, :, h, :], qt_hi[rows].bitcast(F32), ACT.Copy)
                    ins.then_inc(a_qb.sem, 1)
                elif kind == "score":
                    if k >= 2:
                        act.wait_ge(t_o.sem, t_o.after(b, k - 1))
                    act.wait_ge(d_p.sem, d_p.after(b, k + 1))
                    act.activation(p_hi[:, k % 2], p32[:, k % 2], ACT.Copy).then_inc(a_p.sem, 1)
                elif kind == "state":
                    if k >= 2:
                        act.wait_ge(t_o.sem, t_o.after(b, k))
                    act.wait_ge(d_s.sem, d_s.after(b, k + 1))
                    act.activation(s_hi[:, k % 2], s32[:], ACT.Copy).then_inc(a_s.sem, 1)
                elif kind == "o":
                    act.wait_ge(t_o.sem, t_o.after(b, k + 1))
                    act.activation(heads(xn[:, k]), po[k % 2][:, :].rearrange("p (h s v) -> p h s v", h=HEADS, s=2
                                                                              )[:, :, 1], ACT.Copy
                                   ).then_inc(a_o.sem, 1)
                elif kind == "ss":
                    act.wait_ge(d_o.sem, d_o.after(b, k + 1))
                    if k >= 2:
                        act.wait_ge(d_ss.sem, d_ss.after(b, k - 1))
                    act.activation(sq[:, k % 2], xn[:, k], ACT.Square).then_inc(a_sq.sem, 1)
                elif kind == "yt":
                    act.wait_ge(t_yt.sem, t_yt.after(b, k + 1))
                    act.activation(h1_hi[:, :, 2 * k * P:(2 * k + 2) * P],
                                   py[k][:, :].rearrange("p (k n) -> p k n", k=KC), ACT.Copy).then_inc(a_yt.sem, 1)
                elif kind == "h2":
                    tok = slice(2 * k * P, (2 * k + 2) * P)
                    act.wait_ge(d_h2.sem, d_h2.after(b, k + 1))
                    act.activation(h2_hi[:, :, tok], h32[:, :, tok], ACT.Copy).then_inc(a_h2.sem, 1)
                elif kind == "up":
                    act.wait_ge(t_u1.sem, t_u1.after(f, k + 1))
                    if k >= 2:
                        act.wait_ge(d_hid.sem, d_hid.after(f, k - 1))
                    act.activation(silu1[:, k % 2], pu1[:, :], ACT.Silu).then_inc(a_silu.sem, 1)
                elif kind == "hid":
                    act.wait_ge(d_hid.sem, d_hid.after(f, k + 1))
                    if k >= 2:
                        act.wait_ge(t_d.sem, t_d.after(f, k - 1))
                    act.activation(hid_hi[:, k % 2], hid32[:, k % 2], ACT.Copy).then_inc(a_hid.sem, 1)

            run(act, step)

        @block.gpsimd
        def _(pool):
            pool.memset(eps_ln[:], EPS).then_inc(p_mhalf.sem, 1)
            pool.memset(unread[:], 0.0).then_inc(p_out.sem, 1)
            pool.memset(eps_rms[:], DV * EPS).then_inc(p_mhalf.sem, 1)
            pool.memset(mhalf[:], -0.5).then_inc(p_mhalf.sem, 1)

            def step(kind, k, b, f):
                first = b == 0 if isinstance(b, int) else False
                if kind == "stats":
                    m, n = divmod(k, 2)
                    pair = slice(2 * n, 2 * n + 2)
                    pool.wait_ge(p_mhalf.sem, 3)
                    pool.wait_ge(d_mv1.sem, k + 1)
                    pool.tensor_tensor(ve1[:, m, pair], mv1[:, m, pair, 1], eps_ln[:, 0:2], ALU.add
                                       ).then_inc(p_ve1.sem, 1)
                    pool.wait_ge(p_ve1.sem, k + 1)
                    pool.tensor_tensor(rs1[:, m, pair], ve1[:, m, pair], mhalf[:, 0:2], ALU.pow).then_inc(p_rs1.sem, 1)
                elif kind == "zero":
                    pool.wait_ge(t_cols2.sem, 1)
                    pool.wait_ge(t_rows.sem, 1)
                    pool.wait_ge(d_wqkvg.sem, 1)
                    pool.wait_ge(p_wqkvg.sem, 1)
                    pool.memset(qb_hi[:].bitcast(F32), 0.0).then_inc(p_zero.sem, 1)
                    pool.memset(qb_lo[:].bitcast(F32), 0.0).then_inc(p_zero.sem, 1)
                elif kind == "w_lo":
                    pool.wait_ge(a_wqkvg.sem, 1)
                    pool.tensor_tensor(wqkvg_lo[:, 0], stage_qkvg[:, 0], wqkvg_hi[:, 0].bitcast(F32), ALU.subtract
                                       ).then_inc(p_wqkvg.sem, 1)
                elif kind == "w_w13" and k in W13_B:
                    pool.wait_ge(a_w13.sem, k + 1)
                    pool.tensor_tensor(w13_lo[:, k], stage_13[:, k % 2], w13_hi[:, k].bitcast(F32), ALU.subtract
                                       ).then_inc(p_w13.sem, 1)
                elif kind == "fold":
                    pool.wait_ge(a_fly.sem, k + 1)
                    pool.tensor_tensor(w2_lo[:, 2 * k:2 * k + 2], fly1[:, 2 * k:2 * k + 2],
                                       w2_hi[:, 2 * k:2 * k + 2].bitcast(F32), ALU.subtract).then_inc(p_w2lo.sem, 1)
                elif kind == "fly_b":
                    butterfly(pool, k, FLY_B, p_fly)
                elif kind == "qk":
                    pool.wait_ge(d_rope.sem, d_rope.after(b, k + 1))
                    pool.tensor_tensor(qk[:, k], rope_a[:, k % 2], rope_b[:, k % 2], ALU.add
                                       ).then_inc(p_rope.sem, 1)
                elif kind == "vg":
                    if first and k == 0:
                        pool.wait_ge(a_gn.sem, 1)
                    pool.wait_ge(a_vg.sem, a_vg.after(b, k + 1))
                    pool.tensor_tensor(gg[:, k].rearrange("p (h v) -> p h v", h=HEADS),
                                       g32[:, k % 2].rearrange("p (h v) -> p h v", h=HEADS),
                                       gnorm_sb[:].unsqueeze(1).to_broadcast([P, HEADS, DV]), ALU.mult
                                       ).then_inc(p_gg.sem, 1)
                elif kind == "ksplit":
                    pool.wait_ge(a_k.sem, a_k.after(b, 1))
                    pool.tensor_tensor(k_lo[:], qk[:, :, P:2 * P], k_hi[:].bitcast(F32), ALU.subtract
                                       ).then_inc(p_k.sem, 1)
                elif kind == "state":
                    pool.wait_ge(a_s.sem, a_s.after(b, k + 1))
                    pool.tensor_tensor(s_lo[:, k % 2], s32[:], s_hi[:, k % 2].bitcast(F32), ALU.subtract
                                       ).then_inc(p_s.sem, 1)
                elif kind == "ss":
                    pool.wait_ge(a_sq.sem, a_sq.after(b, k + 1))
                    pool.tensor_tensor(xn[:, k], xn[:, k], gg[:, k], ALU.mult).then_inc(p_y0.sem, 1)
                elif kind == "rms":
                    s2, v2, r2 = (t[:, 2 * k:2 * k + 2].rearrange("p t h -> p (t h)") for t in (ss, vo, rso))
                    pool.wait_ge(d_ss.sem, d_ss.after(b, 2 * k + 2))
                    pool.tensor_tensor(v2, s2, eps_rms[:], ALU.add).then_inc(p_vo.sem, 1)
                    pool.wait_ge(p_vo.sem, p_vo.after(b, k + 1))
                    pool.tensor_tensor(r2, v2, mhalf[:], ALU.pow).then_inc(p_rso.sem, 1)
                elif kind == "proj":
                    pair = slice(2 * k, 2 * k + 2)
                    pool.wait_ge(d_mv2.sem, d_mv2.after(b, k + 1))
                    pool.tensor_tensor(ve2[:, pair], mv2[:, pair, 1], eps_ln[:, 0:2], ALU.add).then_inc(p_ve2.sem, 1)
                    pool.wait_ge(p_ve2.sem, p_ve2.after(b, k + 1))
                    pool.tensor_tensor(rs2[:, pair], ve2[:, pair], mhalf[:, 0:2], ALU.pow).then_inc(p_rs2.sem, 1)
                    pool.tensor_tensor(xres[:, b, pair], xres[:, b, pair], branch[k][:], ALU.add
                                       ).then_inc(p_x1.sem, 1)
                elif kind == "hid" and not very_last(f, k):
                    pool.wait_ge(a_hid.sem, a_hid.after(f, k + 1))
                    pool.tensor_tensor(hid_lo[:, k % 2], hid32[:, k % 2], hid_hi[:, k % 2].bitcast(F32),
                                       ALU.subtract).then_inc(p_hid.sem, 1)
                elif kind == "out":
                    pair = slice(2 * k, 2 * k + 2)
                    pool.wait_ge(p_x1.sem, p_x1.after(f, 2))
                    pool.wait_ge(d_fin.sem, d_fin.after(f, k + 1))
                    pool.tensor_tensor(xres[:, f, pair], xres[:, f, pair], hid32[:, k].rearrange(
                        "p (t d) -> p t d", t=2), ALU.add).then_inc(p_out.sem, 1)

            run(pool, step)


def constants():
    i = np.arange(P)
    head = np.arange(QK) % P // DK
    consts = np.zeros((P, C_END), np.float32)
    consts[:, C_IDENT:C_IDENT + P] = np.eye(P)
    consts[:, C_CAUSAL:C_CAUSAL + P] = i[None, :] >= i[:, None]
    bits = np.array([[bin(r & c).count("1") for c in range(P)] for r in range(P)])
    consts[:, C_HADAMARD:C_HADAMARD + P] = 1 - 2 * (bits % 2)
    consts[:, C_BLOCKS:C_END] = i[:, None] // DK == np.arange(HEADS * DV)[None, :] // DV
    select = np.zeros((B, B, P), np.float32)
    for b in range(B):
        select[b, b] = 1
    inv_freq = (np.float32(1) / np.float32(10000) ** (np.arange(0, DK, 2, dtype=np.float32) / np.float32(DK)))
    angle = (np.arange(N, dtype=np.float32)[:, None] * inv_freq.astype(np.float32)).astype(np.float64)
    angle = angle[:, np.arange(QK) % (DK // 2)]
    gamma = 1.0 - 2.0 ** (-5.0 - head)
    is_q = np.arange(QK) < P
    power = np.arange(N)[:, None] * np.where(is_q, 1.0, -1.0)
    factor = gamma ** power * np.where(is_q, DK ** -0.5, 1.0)
    sign = np.where(np.arange(QK) % DK < DK // 2, 1.0, -1.0)
    tile = lambda a: np.ascontiguousarray(a.astype(np.float32).reshape(TILES, P, QK).transpose(1, 0, 2))
    return consts, select, tile(np.cos(angle) * factor), tile(np.sin(angle) * factor * sign)


def rows_to_partitions(w):
    return np.ascontiguousarray(w.reshape(-1, P, w.shape[1]).transpose(1, 0, 2))


def kernel(L0_attn_x, L0_attn_Wq, L0_attn_Wk, L0_attn_Wv, L0_attn_Wg, L0_attn_Wo, L0_attn_gnorm_w,
           L0_ffn_W1, L0_ffn_W2, L0_ffn_W3, L0_c, L0_wmod):
    import concourse.bacc as bacc
    from concourse.bass_utils import run_bass_kernel_spmd

    arr = np.asarray
    w_qkvg = rows_to_partitions(np.concatenate([arr(w) for w in (L0_attn_Wq, L0_attn_Wk, L0_attn_Wv, L0_attn_Wg)]).T)
    w13 = np.stack([rows_to_partitions(arr(w).T) for w in (L0_ffn_W1, L0_ffn_W3)])
    w13 = np.ascontiguousarray(w13.reshape(2, P, KC, PIECES, PW).transpose(3, 1, 0, 2, 4))
    consts, select, cos, sin = constants()
    arrays = {
        "x": arr(L0_attn_x),
        "c_t": rows_to_partitions(arr(L0_c).T),
        "w_qkvg": w_qkvg,
        "w_o": rows_to_partitions(arr(L0_attn_Wo).T),
        "gnorm": np.ascontiguousarray(np.broadcast_to(arr(L0_attn_gnorm_w), (P, DV))),
        "w13": w13,
        "w2": rows_to_partitions(arr(L0_ffn_W2).T),
        "wmod": rows_to_partitions(arr(L0_wmod)),
        "consts": consts, "select": select, "cos": cos, "sin": sin,
    }
    nc = bacc.Bacc("TRN2", target_bir_lowering=False, num_devices=1)
    args = [nc.dram_tensor(name, a.shape, mybir.dt.from_np(a.dtype), kind="ExternalInput").ap()
            for name, a in arrays.items()]
    args.append(nc.dram_tensor("out", (B, N, D), F32, kind="ExternalOutput").ap())
    adaln_block_kernel(nc, *args)
    return run_bass_kernel_spmd(nc, [arrays], core_ids=[0]).results[0]["out"]
```
